# Optimizing a Trainium2 kernel written in Bass

```python
import numpy as np
import jax
import jax.numpy as jnp

def _softmax(x, axis=-1):
    return jax.nn.softmax(x, axis=axis)

def _gelu(x):
    return jax.nn.gelu(x, approximate=True)

def _silu(x):
    return jax.nn.silu(x)

def _sigmoid(x):
    return jax.nn.sigmoid(x)

def _layernorm(x, axis=-1, eps=1e-05):
    m = jnp.mean(x, axis=axis, keepdims=True)
    v = jnp.var(x, axis=axis, keepdims=True)
    return (x - m) / jnp.sqrt(v + eps)

def _scatter_add(tgt, idx, src, axis=0):
    return tgt.at[idx].add(src)

def _segment_sum(src, seg, n):
    return jax.ops.segment_sum(src, seg, n)
kernel_name = 'mk_hybrid_d1_jaxref_r4_10a9f0'

def setup_inputs(seed: int=0):
    np.random.seed(seed)
    _w = jnp.asarray

    def _L0_attn_a_setup():
        import jax, jax.numpy as jnp
        import numpy as np
        EMBED_DIM = 256
        NUM_HEADS = 16
        HEAD_DIM = EMBED_DIM // NUM_HEADS

        def _sinusoid_pos_emb(seq_len, dim):
            pos = jnp.arange(seq_len, dtype=jnp.float32)
            idx = jnp.arange(dim // 2, dtype=jnp.float32)
            inv_freq = 1.0 / 10000.0 ** (2.0 * idx / dim)
            ang = pos[:, None] * inv_freq[None, :]
            return jnp.concatenate([jnp.sin(ang), jnp.cos(ang)], axis=-1)

        def _relative_shift(x):
            b, h, s, _ = x.shape
            x = jnp.pad(x, ((0, 0), (0, 0), (0, 0), (1, 0)))
            x = x.reshape(b, h, s + 1, s)
            return x[:, :, 1:, :].reshape(b, h, s, s)
        key = jax.random.key(seed)
        ks = jax.random.split(key, 12)
        D = EMBED_DIM
        sc = 1.0 / np.sqrt(D)
        inp = {'x': jax.random.normal(ks[0], (2, 512, D), dtype=jnp.float32)}
        for i, name in enumerate(['Wq', 'Wk', 'Wv', 'Wp', 'Wo']):
            inp[name] = jax.random.normal(ks[1 + i], (D, D), dtype=jnp.float32) * sc
            inp['b' + name[1].lower()] = jnp.zeros((D,), dtype=jnp.float32)
        inp['u'] = jax.random.normal(ks[6], (1, NUM_HEADS, 1, HEAD_DIM), dtype=jnp.float32) * 0.05
        inp['v'] = jax.random.normal(ks[7], (1, NUM_HEADS, 1, HEAD_DIM), dtype=jnp.float32) * 0.05
        return inp
    _L0_attn_a_in = _L0_attn_a_setup()

    def _L0_attn_b_setup():
        import jax, jax.numpy as jnp
        import numpy as np
        import math
        B, T, D = (2, 1024, 256)
        H = 16
        HEAD_DIM = D // H
        CHUNK = 64

        def chunked_attention(q, k, v, chunk_size, scale):
            Bq, Hq, Tq, hd = q.shape
            S = k.shape[2]
            nc = Tq // chunk_size
            q_chunks = q.reshape(Bq, Hq, nc, chunk_size, hd).transpose(2, 0, 1, 3, 4)
            starts = jnp.arange(nc, dtype=jnp.int32) * chunk_size
            k_pos = jnp.arange(S)

            def body(carry, xs):
                qc, start = xs
                scores = jnp.einsum('bhqd,bhkd->bhqk', qc, k) * scale
                q_pos = start + jnp.arange(chunk_size)
                causal_mask = k_pos[None, :] > q_pos[:, None]
                scores = jnp.where(causal_mask[None, None], -jnp.inf, scores)
                m = jnp.max(scores, axis=-1, keepdims=True)
                m = jnp.where(jnp.isinf(m), jnp.zeros_like(m), m)
                p = jax.nn.softmax(scores - m, axis=-1)
                oc = jnp.einsum('bhqk,bhkd->bhqd', p, v)
                return (carry, oc)
            _, outs = jax.lax.scan(body, None, (q_chunks, starts))
            return outs.transpose(1, 2, 0, 3, 4).reshape(Bq, Hq, Tq, hd)
        key = jax.random.key(seed)
        ks = jax.random.split(key, 9)
        s = 1.0 / math.sqrt(D)
        return {'x': jax.random.normal(ks[0], (B, T, D), dtype=jnp.float32), 'Wq': jax.random.normal(ks[1], (D, D), dtype=jnp.float32) * s, 'bq': jax.random.normal(ks[2], (D,), dtype=jnp.float32) * 0.01, 'Wk': jax.random.normal(ks[3], (D, D), dtype=jnp.float32) * s, 'bk': jax.random.normal(ks[4], (D,), dtype=jnp.float32) * 0.01, 'Wv': jax.random.normal(ks[5], (D, D), dtype=jnp.float32) * s, 'bv': jax.random.normal(ks[6], (D,), dtype=jnp.float32) * 0.01, 'Wo': jax.random.normal(ks[7], (D, D), dtype=jnp.float32) * s, 'bo': jax.random.normal(ks[8], (D,), dtype=jnp.float32) * 0.01}
    _L0_attn_b_in = _L0_attn_b_setup()

    def _L0_ffn_setup():
        import jax, jax.numpy as jnp
        import numpy as np
        HIDDEN = 256
        INTER = 1024
        key = jax.random.key(seed)
        k1, k2, k3, k4, k5 = jax.random.split(key, 5)
        hidden_states = jax.random.normal(k1, (4, 512, HIDDEN), dtype=jnp.float32)
        W1 = jax.random.normal(k2, (HIDDEN, INTER), dtype=jnp.float32) * (1.0 / np.sqrt(HIDDEN))
        b1 = jax.random.normal(k3, (INTER,), dtype=jnp.float32) * 0.02
        W2 = jax.random.normal(k4, (INTER, HIDDEN), dtype=jnp.float32) * (1.0 / np.sqrt(INTER))
        b2 = jax.random.normal(k5, (HIDDEN,), dtype=jnp.float32) * 0.02
        return {'hidden_states': hidden_states, 'W1': W1, 'b1': b1, 'W2': W2, 'b2': b2}
    _L0_ffn_in = _L0_ffn_setup()
    _d = {'L0_attn_a_x': _L0_attn_a_in['x'], 'L0_attn_a_Wq': _L0_attn_a_in['Wq'], 'L0_attn_a_bq': _L0_attn_a_in['bq'], 'L0_attn_a_Wk': _L0_attn_a_in['Wk'], 'L0_attn_a_bk': _L0_attn_a_in['bk'], 'L0_attn_a_Wv': _L0_attn_a_in['Wv'], 'L0_attn_a_bv': _L0_attn_a_in['bv'], 'L0_attn_a_Wp': _L0_attn_a_in['Wp'], 'L0_attn_a_bp': _L0_attn_a_in['bp'], 'L0_attn_a_Wo': _L0_attn_a_in['Wo'], 'L0_attn_a_bo': _L0_attn_a_in['bo'], 'L0_attn_a_u': _L0_attn_a_in['u'], 'L0_attn_a_v': _L0_attn_a_in['v'], 'L0_attn_b_Wq': _L0_attn_b_in['Wq'], 'L0_attn_b_bq': _L0_attn_b_in['bq'], 'L0_attn_b_Wk': _L0_attn_b_in['Wk'], 'L0_attn_b_bk': _L0_attn_b_in['bk'], 'L0_attn_b_Wv': _L0_attn_b_in['Wv'], 'L0_attn_b_bv': _L0_attn_b_in['bv'], 'L0_attn_b_Wo': _L0_attn_b_in['Wo'], 'L0_attn_b_bo': _L0_attn_b_in['bo'], 'L0_ffn_W1': _L0_ffn_in['W1'], 'L0_ffn_b1': _L0_ffn_in['b1'], 'L0_ffn_W2': _L0_ffn_in['W2'], 'L0_ffn_b2': _L0_ffn_in['b2']}
    _x0 = _d['L0_attn_a_x']
    _d['L0_attn_a_x'] = jax.random.normal(jax.random.fold_in(jax.random.key(seed), 1), (4, 2048, 256), dtype=_x0.dtype)
    del _x0
    return _d

def reference(L0_attn_a_x, L0_attn_a_Wq, L0_attn_a_bq, L0_attn_a_Wk, L0_attn_a_bk, L0_attn_a_Wv, L0_attn_a_bv, L0_attn_a_Wp, L0_attn_a_bp, L0_attn_a_Wo, L0_attn_a_bo, L0_attn_a_u, L0_attn_a_v, L0_attn_b_Wq, L0_attn_b_bq, L0_attn_b_Wk, L0_attn_b_bk, L0_attn_b_Wv, L0_attn_b_bv, L0_attn_b_Wo, L0_attn_b_bo, L0_ffn_W1, L0_ffn_b1, L0_ffn_W2, L0_ffn_b2):

    def _L0_attn_a_ref(x, Wq, bq, Wk, bk, Wv, bv, Wp, bp, Wo, bo, u, v):
        import jax, jax.numpy as jnp
        import numpy as np
        EMBED_DIM = 256
        NUM_HEADS = 16
        HEAD_DIM = EMBED_DIM // NUM_HEADS

        def _sinusoid_pos_emb(seq_len, dim):
            pos = jnp.arange(seq_len, dtype=jnp.float32)
            idx = jnp.arange(dim // 2, dtype=jnp.float32)
            inv_freq = 1.0 / 10000.0 ** (2.0 * idx / dim)
            ang = pos[:, None] * inv_freq[None, :]
            return jnp.concatenate([jnp.sin(ang), jnp.cos(ang)], axis=-1)

        def _relative_shift(x):
            b, h, s, _ = x.shape
            x = jnp.pad(x, ((0, 0), (0, 0), (0, 0), (1, 0)))
            x = x.reshape(b, h, s + 1, s)
            return x[:, :, 1:, :].reshape(b, h, s, s)
        B, S, D = x.shape
        H, P = (NUM_HEADS, HEAD_DIM)

        def heads(t):
            return t.reshape(B, S, H, P).transpose(0, 2, 1, 3)
        q = heads(x @ Wq + bq)
        k = heads(x @ Wk + bk)
        val = heads(x @ Wv + bv)
        pos = _sinusoid_pos_emb(S, D) @ Wp + bp
        pos = pos.reshape(S, H, P).transpose(1, 0, 2)
        content_score = jnp.einsum('bhsp,bhtp->bhst', q + u, k)
        pos_score = jnp.einsum('bhsp,htp->bhst', q + v, pos)
        pos_score = _relative_shift(pos_score)
        score = (content_score + pos_score) / jnp.sqrt(jnp.float32(P))
        weights = jax.nn.softmax(score, axis=-1)
        out = jnp.einsum('bhst,bhtp->bhsp', weights, val)
        out = out.transpose(0, 2, 1, 3).reshape(B, S, D)
        return out @ Wo + bo

    def _L0_attn_b_ref(x, Wq, bq, Wk, bk, Wv, bv, Wo, bo):
        import jax, jax.numpy as jnp
        import numpy as np
        import math
        B, T, D = (2, 1024, 256)
        H = 16
        HEAD_DIM = D // H
        CHUNK = 64

        def chunked_attention(q, k, v, chunk_size, scale):
            Bq, Hq, Tq, hd = q.shape
            S = k.shape[2]
            nc = Tq // chunk_size
            q_chunks = q.reshape(Bq, Hq, nc, chunk_size, hd).transpose(2, 0, 1, 3, 4)
            starts = jnp.arange(nc, dtype=jnp.int32) * chunk_size
            k_pos = jnp.arange(S)

            def body(carry, xs):
                qc, start = xs
                scores = jnp.einsum('bhqd,bhkd->bhqk', qc, k) * scale
                q_pos = start + jnp.arange(chunk_size)
                causal_mask = k_pos[None, :] > q_pos[:, None]
                scores = jnp.where(causal_mask[None, None], -jnp.inf, scores)
                m = jnp.max(scores, axis=-1, keepdims=True)
                m = jnp.where(jnp.isinf(m), jnp.zeros_like(m), m)
                p = jax.nn.softmax(scores - m, axis=-1)
                oc = jnp.einsum('bhqk,bhkd->bhqd', p, v)
                return (carry, oc)
            _, outs = jax.lax.scan(body, None, (q_chunks, starts))
            return outs.transpose(1, 2, 0, 3, 4).reshape(Bq, Hq, Tq, hd)
        Bx, Tx, Dx = x.shape
        scale = 1.0 / math.sqrt(HEAD_DIM)

        def proj(W, b):
            y = x @ W.T + b
            return y.reshape(Bx, Tx, H, HEAD_DIM).transpose(0, 2, 1, 3)
        q = proj(Wq, bq)
        k = proj(Wk, bk)
        v = proj(Wv, bv)
        out = chunked_attention(q, k, v, CHUNK, scale)
        out = out.transpose(0, 2, 1, 3).reshape(Bx, Tx, Dx)
        return out @ Wo.T + bo

    def _L0_ffn_ref(hidden_states, W1, b1, W2, b2):
        import jax, jax.numpy as jnp
        import numpy as np
        HIDDEN = 256
        INTER = 1024
        h = jax.nn.relu(jnp.einsum('bsh,hi->bsi', hidden_states, W1) + b1)
        return jnp.einsum('bsi,ih->bsh', h, W2) + b2
    x = L0_attn_a_x
    x = x + _L0_attn_a_ref(_layernorm(x, axis=-1), L0_attn_a_Wq, L0_attn_a_bq, L0_attn_a_Wk, L0_attn_a_bk, L0_attn_a_Wv, L0_attn_a_bv, L0_attn_a_Wp, L0_attn_a_bp, L0_attn_a_Wo, L0_attn_a_bo, L0_attn_a_u, L0_attn_a_v)
    x = x + _L0_ffn_ref(_layernorm(x, axis=-1), L0_ffn_W1, L0_ffn_b1, L0_ffn_W2, L0_ffn_b2)
    x = x + _L0_attn_b_ref(_layernorm(x, axis=-1), L0_attn_b_Wq, L0_attn_b_bq, L0_attn_b_Wk, L0_attn_b_bk, L0_attn_b_Wv, L0_attn_b_bv, L0_attn_b_Wo, L0_attn_b_bo)
    x = x + _L0_ffn_ref(_layernorm(x, axis=-1), L0_ffn_W1, L0_ffn_b1, L0_ffn_W2, L0_ffn_b2)
    return x

_drawn_inputs = setup_inputs


def setup_inputs(seed=0):
    import zlib

    import numpy as np

    out = dict(_drawn_inputs(seed))
    spreads = {'L0_attn_a_bq': (0.0, 0.8),
     'L0_attn_a_bk': (0.0, 2.0),
     'L0_attn_a_bv': (0.0, 0.1),
     'L0_attn_a_bp': (0.0, 2.0),
     'L0_attn_a_bo': (0.0, 0.1)}
    factors = {'L0_attn_a_u': 8.0,
     'L0_attn_a_v': 27.789,
     'L0_attn_b_bq': 64.0,
     'L0_attn_b_bk': 64.0,
     'L0_attn_b_bv': 8.0,
     'L0_attn_b_bo': 8.0,
     'L0_ffn_b1': 3.398}
    for name, (base, spread) in spreads.items():
        noise = np.random.default_rng([zlib.crc32(name.encode()), seed]).standard_normal(out[name].shape)
        drawn = base * np.exp(spread * noise) if base else spread * noise
        out[name] = jnp.asarray(drawn.astype(out[name].dtype))
    for name, factor in factors.items():
        out[name] = (out[name] * factor).astype(out[name].dtype)
    return out
```

```python
from contextlib import ExitStack

import numpy as np

import concourse.bass as bass
from concourse import mybir

F32 = mybir.dt.float32
BF16 = mybir.dt.bfloat16
ALU = mybir.AluOpType
ACT = mybir.ActivationFunctionType
AX = mybir.AxisListType

P = 128
D = 256
KT = D // P
H = 16
HD = D // H
S = 2048
NT = S // P
CH = 512
NC = S // CH
INTER = 1024
NI = INTER // P
PARTS = 3
SLOTS = 6
KROWS = SLOTS * HD
STRIP = S + P
RING = 4
AHEAD = 4
VW = 32
SCALE = 1.0 / float(np.sqrt(HD))
EPS = 1e-5
NEG = -1.0e30

R_CHUNKS = [(c * CH, min(CH, STRIP - c * CH)) for c in range(5)]
R_BANK = [0, 1, 2, 0, 1]
R_BY_DVE = [3]
P_BANK = [2, 0, 1, 2]
P_BY_DVE = [2, 3]
B_BANK = [0, 1, 2, 0]

COLS = dict(bq=0, bk=2, bp=4, u=6, v=8, Bbq=10, Bbk=12, b1=14)
NCOLS = 22
ROWS = dict(bv=0, bo=1, Bbv=2, Bbo=3, b2=4)


def program(nc, a, out, nb=4, nh=H):
    ctx = ExitStack()
    with ctx:
        def sb(name, shape, dt=F32):
            return ctx.enter_context(nc.sbuf_tensor(name, shape, dt))

        def pb(name, shape):
            return ctx.enter_context(nc.psum_tensor(name, shape, F32))

        def sem(name):
            return ctx.enter_context(nc.semaphore(name))

        qu_d = nc.dram_tensor("qu_parts", (H + 1, PARTS * HD, S), BF16).ap()
        qv_d = nc.dram_tensor("qv_parts", (H + 1, PARTS * HD, S), BF16).ap()
        k_d = nc.dram_tensor("k_parts", (H + 1, PARTS * HD, S), BF16).ap()
        pos_d = nc.dram_tensor("pos_parts", (H + 1, PARTS * HD, S), BF16).ap()
        v_d = nc.dram_tensor("v_heads", (H + 1, P, NT * VW), F32).ap()
        strip_d = nc.dram_tensor("strips", (RING, P, STRIP), F32).ap()

        x_res = sb("x_res", [P, NT, D])
        xnT = sb("xnT", [P, KT, S])
        attn = sb("attn", [P, NT, D])
        qu_s = sb("qu_s", [KROWS, S], BF16)
        k_s = sb("k_s", [KROWS, S], BF16)
        qv_s = sb("qv_s", [KROWS, S + 1], BF16)
        pos_s = sb("pos_s", [KROWS, S + 1], BF16)
        v_s = sb("v_s", [P, NT, VW])
        strips = sb("strips_sb", [P, RING * STRIP])
        z = sb("z", [P, RING, S])
        pT = sb("pT", [P, 2, S])
        po_sb = sb("po_sb", [P, P])
        rsum = sb("rsum", [P, 1])
        mlo = sb("mlo", [P, 2])
        mhi = sb("mhi", [P, 2])
        nmax = sb("nmax", [P, 2])
        idle = sb("idle", [P, 1])
        wA = sb("wA", [P, 4, KT, D])
        wB = sb("wB", [P, 4, KT, D])
        wp = sb("wp", [P, KT, D])
        w1 = sb("w1", [P, KT, INTER])
        w2 = sb("w2", [P, NI, D])
        cols = sb("cols", [P, NCOLS])
        rows = sb("rows", [P, 5, D])
        ident = sb("ident", [P, P])
        sel = sb("sel", [P, VW])
        mask = sb("mask", [P, S])
        bqu = sb("bqu", [P, KT])
        bqv = sb("bqv", [P, KT])
        stats = sb("stats", [P, NT, 6])
        mv = sb("mv", [P, NT, 2])
        ve = sb("ve", [P, NT])
        rstd = sb("rstd", [P, NT])
        nwt = sb("nwt", [P, 3, NT])
        xn = sb("xn", [P, 2, D])
        aoT = sb("aoT", [P, 2, KT, P])

        zf = z[:, :, :].rearrange("p r s -> p (r s)")
        zb = zf.bitcast(BF16)
        parts = [[zb[:, (2 * 3 + 0) * 0 + (s * 3 + i) * S:(s * 3 + i + 1) * S] for i in range(PARTS)] for s in range(2)]
        resid = [zf[:, 3 * S + i * CH:3 * S + (i + 1) * CH] for i in range(4)]
        v_all = strips[:, 0:H * NT * VW].rearrange("p (h t w) -> p h t w", h=H, t=NT)
        hT = [strips[:, i * NI * CH:(i + 1) * NI * CH].rearrange("p (n c) -> p n c", n=NI) for i in range(2)]
        embT = strips[:, 0:KT * S].rearrange("p (k s) -> p k s", k=KT)

        sc = pb("sc", [P, 4, CH])
        rg = pb("rg", [P, 3, CH])
        op = pb("op", [P, CH])
        po = op[:, 0:P]
        on = op[:, P:P + VW]
        scf = sc[:, :, :].rearrange("p b c -> p (b c)")

        phase_done = sem("phase_done")
        waited = sem("waited")
        loaded = sem("loaded")
        zeroed = sem("zeroed")
        bias_ready = sem("bias_ready")
        x_loaded = sem("x_loaded")
        stored = sem("stored")
        ln_stat = sem("ln_stat")
        ln_var = sem("ln_var")
        ln_sqrt = sem("ln_sqrt")
        ln_step = sem("ln_step")
        ln_xn = sem("ln_xn")
        ln_tr = sem("ln_tr")
        ln_out = sem("ln_out")
        pj_ready = sem("pj_ready")
        pj_high = sem("pj_high")
        pj_resid = sem("pj_resid")
        pj_mid = sem("pj_mid")
        pj_low = sem("pj_low")
        pj_stored = [sem("pj_stored0"), sem("pj_stored1")]
        pv_ready = sem("pv_ready")
        pv_added = sem("pv_added")
        pv_pad = sem("pv_pad")
        pv_stored = sem("pv_stored")
        oo_tr = sem("oo_tr")
        oo_T = sem("oo_T")
        oo_ready = sem("oo_ready")
        oo_sum = sem("oo_sum")
        oo_added = sem("oo_added")
        ff_h = sem("ff_h")
        ff_relu = sem("ff_relu")
        ff_ready = sem("ff_ready")
        ff_sum = sem("ff_sum")
        ff_added = sem("ff_added")
        names = ["lo_ready", "hi_ready", "lo_read", "hi_read", "maxes", "nmax_ready", "exp_done", "pv_done",
                 "po_copied", "comb_done", "rcp", "out_read", "qk_loaded", "v_loaded"]
        AA = {n: sem("A_" + n) for n in names}
        BB = {n: sem("B_" + n) for n in names}
        for q in range(4):
            AA[f"pt_full{q}"] = sem(f"A_pt_full{q}")
            AA[f"pt_free{q}"] = sem(f"A_pt_free{q}")
        for n in ("pt_full", "pt_by_act", "pt_by_dve"):
            BB[n] = sem("B_" + n)
        r_full = [sem(f"r_full{c}") for c in range(5)]
        r_free = [sem(f"r_free{c}") for c in range(5)]
        strip_out = [sem(f"strip_out{k}") for k in range(RING)]
        strip_in = [sem(f"strip_in{k}") for k in range(RING)]
        qv_loaded = sem("qv_loaded")
        sem_zero = sem("spare_head_zero")

        NPH = 12
        ENG = 5
        LOADS = 17
        QK_INC = 16 * (3 + 6)

        def meet(e, b, k):
            e.drain().then_inc(phase_done, 1)
            e.wait_ge(phase_done, ENG)

        def settle(e):
            e.sem_inc(waited, 1)

        def meet_b(e, b, k):
            v = e.snap(b * (ENG * 13) + ENG * (k + 1))
            settle(e)
            e.drain().then_inc(phase_done, 1)
            e.wait_ge(phase_done, v)
            settle(e)

        def jobs(kind):
            if kind == "pos":
                return [(wp[:, :, :], cols[:, COLS["bp"] + m:COLS["bp"] + m + 1], pos_d, m) for m in range(KT)]
            if kind == "A":
                return ([(wA[:, 0], bqu[:, m:m + 1], qu_d, m) for m in range(KT)]
                        + [(wA[:, 0], bqv[:, m:m + 1], qv_d, m) for m in range(KT)]
                        + [(wA[:, 1], cols[:, COLS["bk"] + m:COLS["bk"] + m + 1], k_d, m) for m in range(KT)])
            return ([(wB[:, 0], cols[:, COLS["Bbq"] + m:COLS["Bbq"] + m + 1], qu_d, m) for m in range(KT)]
                    + [(wB[:, 1], cols[:, COLS["Bbk"] + m:COLS["Bbk"] + m + 1], k_d, m) for m in range(KT)])

        NJ = {"pos": 2, "A": 6, "B": 4}
        JB = NJ["A"] + NJ["B"]
        JOFF = {"pos": 0, "A": NJ["pos"], "B": NJ["pos"] + NJ["A"]}

        def jbase(b, kind):
            return JOFF[kind] if kind == "pos" else b * JB + JOFF[kind]

        def times(x, k):
            return x * k

        def pe_project(e, b, kind, src):
            jb = jbase(b, kind)
            for j, (w, _, _, m) in enumerate(jobs(kind)):
                for c in range(NC):
                    n = j * NC + c
                    if kind == "pos" and n < 4:
                        pass
                    else:
                        if n >= 4:
                            e.wait_ge(pj_resid, jb * NC + (n - 3))
                    for k in range(KT):
                        mm = e.matmul(sc[:, c, :], w[:, k, m * P:(m + 1) * P], src[:, k, c * CH:(c + 1) * CH],
                                      start=k == 0, stop=k == KT - 1)
                    mm.then_inc(pj_ready, 1)

        def act_project(e, b, kind):
            jb = jbase(b, kind)
            for j, (_, bias, _, m) in enumerate(jobs(kind)):
                if j >= 2:
                    e.wait_ge(pj_stored[j % 2], pj_count(b, kind, j - 2))
                for c in range(NC):
                    n = j * NC + c
                    e.wait_ge(pj_ready, jb * NC + (n + 1))
                    e.activation(parts[j % 2][0][:, c * CH:(c + 1) * CH], sc[:, c, :], ACT.Identity,
                                 bias=bias).then_inc(pj_high, 1)

        def dve_project(e, b, kind):
            jb = jbase(b, kind)
            for j, (_, bias, _, m) in enumerate(jobs(kind)):
                for c in range(NC):
                    n = j * NC + c
                    e.wait_ge(pj_high, jb * NC + (n + 1))
                    if n >= 4:
                        e.wait_ge(pj_low, jb * NC + (n - 3))
                    e.scalar_tensor_tensor(out=resid[c], in0=sc[:, c, :], scalar=bias,
                                           in1=parts[j % 2][0][:, c * CH:(c + 1) * CH],
                                           op0=ALU.add, op1=ALU.subtract).then_inc(pj_resid, 1)

        def pool_project(e, b, kind):
            jb = jbase(b, kind)
            for j in range(NJ[kind]):
                if j >= 2:
                    e.wait_ge(pj_stored[j % 2], pj_count(b, kind, j - 2))
                for c in range(NC):
                    n = j * NC + c
                    cs = slice(c * CH, (c + 1) * CH)
                    e.wait_ge(pj_resid, jb * NC + (n + 1))
                    settle(e)
                    e.tensor_copy(parts[j % 2][1][:, cs], resid[c]).then_inc(pj_mid, 1)
                    e.wait_ge(pj_mid, jb * NC + (n + 1))
                    e.tensor_tensor(parts[j % 2][2][:, cs], resid[c], parts[j % 2][1][:, cs],
                                    ALU.subtract).then_inc(pj_low, 1)

        def pj_count(b, kind, j):
            js = (j // 2 + 1)
            off = JOFF[kind] // 2
            per = 16 * PARTS
            return per * (off + js) if kind == "pos" else b * (per * (JB // 2)) + per * (off + js)

        def sp_project(e, b, kind):
            jb = jbase(b, kind)
            for j, (_, _, dst, m) in enumerate(jobs(kind)):
                e.wait_ge(pj_low, jb * NC + (j + 1) * NC)
                settle(e)
                hs = dst[m * (H // KT):(m + 1) * (H // KT), :, :].rearrange("h (a d) s -> a h d s", a=PARTS)
                for i in range(PARTS):
                    e.dma_start(hs[i], parts[j % 2][i]).then_inc(pj_stored[j % 2], 16)
            for j in (NJ[kind] - 2, NJ[kind] - 1):
                e.wait_ge(pj_stored[j % 2], pj_count(b, kind, j))
                settle(e)

        def vcount(b, kind, per):
            return b * (2 * per) + (per if kind == "B" else 0)

        def pe_values(e, b, kind):
            w = wA if kind == "A" else wB
            base = vcount(b, kind, NT)
            for t in range(NT):
                if t >= 3:
                    e.wait_ge(pv_added, base + (t - 2))
                for k in range(KT):
                    mm = e.matmul(rg[:, t % 3, 0:D], xnT[:, k, t * P:(t + 1) * P], w[:, 2, k, :],
                                  start=k == 0, stop=k == KT - 1)
                mm.then_inc(pv_ready, 1)

        def dve_values(e, b, kind):
            bv = rows[:, ROWS["bv" if kind == "A" else "Bbv"], :].rearrange("p (h d) -> p h d", h=H)
            base = vcount(b, kind, NT)
            for t in range(NT):
                e.wait_ge(pv_ready, base + (t + 1))
                e.tensor_tensor(v_all[:, :, t, 0:HD], rg[:, t % 3, 0:D].rearrange("p (h d) -> p h d", h=H), bv,
                                ALU.add).then_inc(pv_added, 1)

        def pool_values(e, b, kind):
            e.memset(v_all[:, :, :, HD + 1:VW], 0.0).then_inc(pv_pad, 1)
            e.memset(v_all[:, :, :, HD:HD + 1], 1.0).then_inc(pv_pad, 1)

        def sp_values(e, b, kind):
            e.wait_ge(pv_added, vcount(b, kind, NT) + NT)
            settle(e)
            e.wait_ge(pv_pad, vcount(b, kind, 2) + 2)
            e.dma_start(v_d[0:H].rearrange("h p w -> p h w"),
                        strips[:, 0:H * NT * VW].rearrange("p (h w) -> p h w", h=H)).then_inc(pv_stored, 16)
            e.wait_ge(pv_stored, vcount(b, kind, 16) + 16)

        def lc(b, k, per):
            return b * (4 * per) + k * per

        def dve_norm(e, b, k):
            for t in range(NT):
                e.bn_stats(stats[:, t, :], x_res[:, t, :]).then_inc(ln_stat, 1)
            for t in range(NT):
                e.wait_ge(ln_stat, lc(b, k, NT) + (t + 1))
                settle(e)
                e.bn_aggr(mv[:, t, :], stats[:, t, :]).then_inc(ln_var, 1)
            e.wait_ge(ln_var, lc(b, k, NT) + NT)
            base = lc(b, k, 6)
            e.tensor_scalar(ve[:, :], mv[:, :, 1], EPS, None, ALU.add).then_inc(ln_step, 1)
            e.wait_ge(ln_sqrt, lc(b, k, 1) + 1)
            e.reciprocal(nwt[:, 1, :], nwt[:, 0, :]).then_inc(ln_step, 1)
            e.wait_ge(ln_step, base + 2)
            e.tensor_tensor(nwt[:, 2, :], nwt[:, 1, :], nwt[:, 1, :], ALU.mult).then_inc(ln_step, 1)
            e.wait_ge(ln_step, base + 3)
            e.tensor_tensor(nwt[:, 2, :], nwt[:, 2, :], ve[:, :], ALU.mult).then_inc(ln_step, 1)
            e.wait_ge(ln_step, base + 4)
            e.tensor_scalar(nwt[:, 2, :], nwt[:, 2, :], -0.5, 1.5, ALU.mult, ALU.add).then_inc(ln_step, 1)
            e.wait_ge(ln_step, base + 5)
            e.tensor_tensor(rstd[:, :], nwt[:, 2, :], nwt[:, 1, :], ALU.mult).then_inc(ln_step, 1)
            e.wait_ge(ln_step, base + 6)
            for t in range(NT):
                if t >= 2:
                    e.wait_ge(ln_tr, lc(b, k, NT) + (t - 1))
                e.tensor_scalar(xn[:, t % 2, :], x_res[:, t, :], mv[:, t, 0:1], rstd[:, t:t + 1],
                                ALU.subtract, ALU.mult).then_inc(ln_xn, 1)

        def act_norm(e, b, k):
            e.wait_ge(ln_step, lc(b, k, 6) + 1)
            e.activation(nwt[:, 0, :], ve[:, :], ACT.Sqrt).then_inc(ln_sqrt, 1)
            for t in range(NT):
                e.wait_ge(ln_tr, lc(b, k, NT) + (t + 1))
                e.activation(xnT[:, :, t * P:(t + 1) * P], rg[:, t % 3, 0:D].rearrange("p (k c) -> p k c", k=KT),
                             ACT.Copy).then_inc(ln_out, 1)

        def pe_norm(e, b, k):
            for t in range(NT):
                e.wait_ge(ln_xn, lc(b, k, NT) + (t + 1))
                if t >= 3:
                    e.wait_ge(ln_out, lc(b, k, NT) + (t - 2))
                for m in range(KT):
                    mm = e.transpose(rg[:, t % 3, m * P:(m + 1) * P], xn[:, t % 2, m * P:(m + 1) * P], ident[:, :])
                mm.then_inc(ln_tr, 1)

        def pe_attention(e, b, kind):
            s_ = AA if kind == "A" else BB

            def strip(t, rb, qv_at):
                i0 = (t % NT) * P
                edge = i0 + P
                if t in (0, NT):
                    e.wait_ge(qv_loaded, qv_at)
                for c, (c0, w) in enumerate(R_CHUNKS):
                    bank = R_BANK[c]
                    claim(bank)
                    for lo, hi, first in ((c0, min(c0 + w, edge), True), (max(c0, edge), c0 + w, False)):
                        if lo >= hi:
                            continue
                        if first:
                            q = qv_s[:, i0:i0 + P]
                            m0 = 1 + S - P - i0 + lo
                        else:
                            q = qv_s[:, i0 + 1:i0 + P + 1]
                            m0 = lo - edge
                        mm = e.matmul(rg[:, bank, lo - c0:hi - c0], q, pos_s[:, m0:m0 + hi - lo],
                                      start=True, stop=True)
                    mm.then_inc(r_full[c], 1)
                    last[bank] = (r_free[c], rb + (t + 1))

            last = {}

            def claim(bank):
                if bank in last:
                    e.wait_ge(*last.pop(bank))

            if kind == "A":
                rb = e.snap(b * (nh * NT + AHEAD))
                for t in range(AHEAD):
                    strip(t, rb, b * (QK_INC * (nh + 1)) + QK_INC)
                for bank in range(3):
                    claim(bank)
                settle(e)

            with e.Fori(0, nh) as h:
                T = e.snap(b * (nh * NT) + h * NT)
                last.clear()
                if kind == "A":
                    rb = e.snap(b * (nh * NT + AHEAD) + h * NT)
                    ql = e.snap(b * (QK_INC * (nh + 1)) + h * QK_INC + 2 * QK_INC)
                for s in range(NT + 2):
                    if s == 0:
                        e.wait_ge(s_["qk_loaded"], b * (QK_INC * (nh + 1)) + h * QK_INC + QK_INC)
                    if s == 2:
                        e.wait_ge(s_["v_loaded"], b * (16 * (nh + 1)) + h * 16 + 16)
                    if s >= 2:
                        t = s - 2
                        if kind == "A":
                            e.wait_ge(s_["pt_free1"], T + (t + 1))
                            e.wait_ge(s_["pt_free3"], T + (t + 1))
                        else:
                            e.wait_ge(s_["pt_by_act"], T + (t + 1))
                            e.wait_ge(s_["pt_by_dve"], T + (t + 1))
                        if t >= 1:
                            e.wait_ge(s_["out_read"], T + t)
                        nj = NT if kind == "A" else t + 1
                        nj4 = max(nj, 4) if kind == "A" else nj
                        for j in range(nj4):
                            g = j % 4
                            mm = e.matmul(po[32 * g:32 * g + 32, :], v_s[:, j, :], pT[:, t % 2, j * P:(j + 1) * P],
                                          start=j < 4, stop=j + 4 >= nj)
                        mm.then_inc(s_["pv_done"], 1)
                    if kind == "A" and s < NT:
                        strip(s + AHEAD, rb, ql)
                    if s < NT:
                        width = S if kind == "A" else (s + 1) * P
                        for half, ready, read in ((0, "lo_ready", "lo_read"), (1, "hi_ready", "hi_read")):
                            if s >= 1 and (kind == "A" or half == 0 or s >= 9):
                                e.wait_ge(s_[read], hcount(kind, T, h, b, half, s))
                            c0s = [c for c in (2 * half, 2 * half + 1) if c * CH < width]
                            for c in c0s:
                                w = min(CH, width - c * CH)
                                mm = e.matmul(sc[:, c, 0:w], qu_s[:, s * P:(s + 1) * P], k_s[:, c * CH:c * CH + w],
                                              start=True, stop=True)
                            if c0s:
                                mm.then_inc(s_[ready], 1)
                    if s >= 2:
                        t = s - 2
                        ng = 4 if kind == "A" else min(4, t + 1)
                        e.wait_ge(s_["po_copied"], T + (t + 1))
                        e.matmul(on, po_sb[0:32 * ng, :], sel[0:32 * ng, :], start=True,
                                 stop=True).then_inc(s_["comb_done"], 1)
                    if 1 <= s <= NT:
                        t = s - 1
                        e.wait_ge(s_["exp_done"], T + (t + 1))
                        nblk = NT if kind == "A" else t + 1
                        if kind == "B" and t >= 1:
                            e.wait_ge(s_["pt_by_act"], T + t)
                            e.wait_ge(s_["pt_by_dve"], T + t)
                        for q in range(4):
                            blks = range(4 * q, min(4 * q + 4, nblk))
                            if not len(blks):
                                continue
                            if kind == "A":
                                bank = P_BANK[q]
                                claim(bank)
                            else:
                                bank = B_BANK[q]
                                if q == 3:
                                    e.wait_ge(pt_first, b * (nh * 4) + h * 4 + (t - 11))
                            for j in blks:
                                mm = e.transpose(rg[:, bank, (j - 4 * q) * P:(j - 4 * q + 1) * P],
                                                 z[:, t % RING, j * P:(j + 1) * P], ident[:, :])
                            if kind == "A":
                                mm.then_inc(s_[f"pt_full{q}"], 1)
                                last[bank] = (s_[f"pt_free{q}"], T + (t + 1))
                            elif q == 2 and nblk > 12:
                                mm.then_inc(pt_three, 1)
                        if kind == "B":
                            mm.then_inc(s_["pt_full"], 1)

        pt_first = sem("B_pt_first")
        pt_three = sem("B_pt_three")

        def hcount(kind, T, h, b, half, s):
            if kind == "A" or half == 0:
                return T + s
            return b * (nh * 8) + h * 8 + (s - 8)

        def hready(kind, T, h, b, half, s):
            if kind == "A" or half == 0:
                return T + (s + 1)
            return b * (nh * 8) + h * 8 + (s - 7)

        def move_strip(e, op_copy, c, t, rb, wb):
            c0, w = R_CHUNKS[c]
            e.wait_ge(r_full[c], rb + (t + 1))
            if t >= RING and (c == 3 or c == 0):
                e.wait_ge(strip_out[t % RING], wb + 16 * (t // RING))
            k = t % RING
            op_copy(strips[:, k * STRIP + c0:k * STRIP + c0 + w], rg[:, R_BANK[c], 0:w]).then_inc(r_free[c], 1)

        def act_copy(e):
            return lambda o, i: e.activation(o, i, ACT.Copy)

        def act_attention(e, b, kind):
            s_ = AA if kind == "A" else BB
            if kind == "A":
                rb = e.snap(b * (nh * NT + AHEAD))
                for t in range(AHEAD):
                    for c in range(5):
                        if c not in R_BY_DVE:
                            move_strip(e, act_copy(e), c, t, rb, 0)
            with e.Fori(0, nh) as h:
                T = e.snap(b * (nh * NT) + h * NT)
                if kind == "A":
                    rb = e.snap(b * (nh * NT + AHEAD) + h * NT)
                    wb = e.snap(b * (16 * (nh * 4 + 1)) + h * 64)
                for s in range(NT + 1):
                    if kind == "A" and s < NT:
                        for c in range(5):
                            if c not in R_BY_DVE:
                                move_strip(e, act_copy(e), c, s + AHEAD, rb, wb)
                    if s >= 1:
                        t = s - 1
                        if t >= 2:
                            e.wait_ge(s_["pv_done"], T + (t - 1))
                        if kind == "A":
                            for q in range(4):
                                if q in P_BY_DVE:
                                    continue
                                e.wait_ge(s_[f"pt_full{q}"], T + (t + 1))
                                e.activation(pT[:, t % 2, q * CH:(q + 1) * CH], rg[:, P_BANK[q], :],
                                             ACT.Copy).then_inc(s_[f"pt_free{q}"], 1)
                        else:
                            nblk = t + 1
                            n4 = t - 11
                            if nblk > 12:
                                e.wait_ge(pt_three, b * (nh * 4) + h * 4 + n4)
                            else:
                                e.wait_ge(s_["pt_full"], T + (t + 1))
                            w = min(CH, nblk * P)
                            mm = e.activation(pT[:, t % 2, 0:w], rg[:, 0, 0:w], ACT.Copy)
                            if nblk > 12:
                                mm.then_inc(pt_first, 1)
                                e.wait_ge(s_["pt_full"], T + (t + 1))
                                w = nblk * P - 3 * CH
                                mm = e.activation(pT[:, t % 2, 3 * CH:3 * CH + w], rg[:, 0, 0:w], ACT.Copy)
                            mm.then_inc(s_["pt_by_act"], 1)
                    if s < NT:
                        w = S if kind == "A" else (s + 1) * P
                        e.wait_ge(s_["nmax_ready"], T + (s + 1))
                        e.activation(z[:, s % RING, 0:w], z[:, s % RING, 0:w], ACT.Exp,
                                     bias=nmax[:, s % 2:s % 2 + 1], scale=SCALE).then_inc(s_["exp_done"], 1)

        def dve_attention(e, b, kind):
            s_ = AA if kind == "A" else BB
            if kind == "A":
                rb = e.snap(b * (nh * NT + AHEAD))
                for t in range(AHEAD):
                    move_strip(e, e.tensor_copy, 3, t, rb, 0)
            with e.Fori(0, nh) as h:
                T = e.snap(b * (nh * NT) + h * NT)
                if kind == "A":
                    rb = e.snap(b * (nh * NT + AHEAD) + h * NT)
                    wb = e.snap(b * (16 * (nh * 4 + 1)) + h * 64)
                    lb = e.snap(b * (16 * (nh * 4 + 1)) + h * 64)
                for s in range(NT + 2):
                    if s >= 2:
                        t = s - 2
                        ng = 4 if kind == "A" else min(4, t + 1)
                        e.wait_ge(s_["pv_done"], T + (t + 1))
                        e.tensor_copy(po_sb[0:32 * ng, :], po[0:32 * ng, :]).then_inc(s_["po_copied"], 1)
                    if kind == "A" and s < NT:
                        move_strip(e, e.tensor_copy, 3, s + AHEAD, rb, wb)
                    if s < NT:
                        width = S if kind == "A" else (s + 1) * P
                        if kind == "A":
                            e.wait_ge(strip_in[s % RING], lb + 16 * (s // RING + 1))
                        elif s >= RING:
                            e.wait_ge(s_["pt_full"], T + (s - RING + 1))
                        lo, hi = mlo[:, s % 2:s % 2 + 1], mhi[:, s % 2:s % 2 + 1]
                        if s >= 2:
                            e.wait_ge(s_["nmax_ready"], T + (s - 1))
                        halves = [(0, "lo_ready", "lo_read", lo), (1, "hi_ready", "hi_read", hi)]
                        halves = [x for x in halves if x[0] * 2 * CH < width]
                        for half, ready, read, mx in halves:
                            c0 = half * 2 * CH
                            c1 = min(width, c0 + 2 * CH)
                            e.wait_ge(s_[ready], hready(kind, T, h, b, half, s))
                            settle(e)
                            zs = z[:, s % RING, c0:c1]
                            add = zs if kind == "A" else mask[:, S - width + c0:S - width + c1]
                            e.tensor_tensor_reduce(out=zs, in0=scf[:, c0:c1], in1=add, scale=1.0, scalar=-3.0e38,
                                                   op0=ALU.add, op1=ALU.max, accum_out=mx).then_inc(s_[read], 1)
                        nm = nmax[:, s % 2:s % 2 + 1]
                        e.wait_ge(s_["lo_read"], T + (s + 1))
                        if s >= 2:
                            e.wait_ge(s_["exp_done"], T + (s - 1))
                        if len(halves) == 2:
                            e.wait_ge(s_["hi_read"], hready(kind, T, h, b, 1, s))
                            e.tensor_scalar(nm, lo, hi, -SCALE, ALU.max,
                                            ALU.mult).then_inc(s_["nmax_ready"], 1)
                        else:
                            e.tensor_scalar(nm, lo, -SCALE, None, ALU.mult).then_inc(s_["nmax_ready"], 1)
                    if s >= 2:
                        t = s - 2
                        e.wait_ge(s_["comb_done"], T + (t + 1))
                        e.reciprocal(rsum[:, :], on[:, HD:HD + 1]).then_inc(s_["rcp"], 1)
                        e.wait_ge(s_["rcp"], T + (t + 1))
                        e.tensor_scalar(attn[:, t, bass.ds(h * HD, HD)], on[:, 0:HD], rsum[:, 0:1], None,
                                        ALU.mult).then_inc(s_["out_read"], 1)
                    if 1 <= s <= NT:
                        t = s - 1
                        if t >= 2:
                            e.wait_ge(s_["pv_done"], T + (t - 1))
                        if kind == "A":
                            for q in P_BY_DVE:
                                e.wait_ge(s_[f"pt_full{q}"], T + (t + 1))
                                e.tensor_copy(pT[:, t % 2, q * CH:(q + 1) * CH],
                                              rg[:, P_BANK[q], :]).then_inc(s_[f"pt_free{q}"], 1)
                        else:
                            nblk = t + 1
                            e.wait_ge(s_["pt_full"], T + (t + 1))
                            w = min(nblk * P, 3 * CH) - CH
                            if w > 0:
                                e.tensor_copy(pT[:, t % 2, CH:CH + w],
                                              rg[:, 1:3, :].rearrange("p b c -> p (b c)")[:, 0:w]).then_inc(
                                                  s_["pt_by_dve"], 1)
                            else:
                                e.memset(idle[:, :], 0.0).then_inc(s_["pt_by_dve"], 1)

        def load_parts(e, dst, col0, src, h, keys, done):
            at = 0
            for first, reps, n in (((0, 3, 1), (1, 2, 1), (2, 1, 1)) if keys else ((0, 1, 3), (0, 1, 2), (0, 1, 1))):
                rows_ = reps * n * HD
                s2 = src[bass.ds(h, 1), first * HD:(first + n) * HD, :].rearrange("a r s -> (a r) s")
                if keys:
                    for r in range(reps):
                        e.dma_start(dst[at:at + HD, col0:col0 + S], s2).then_inc(done, 16)
                        at += HD
                else:
                    e.dma_start(dst[at:at + rows_, col0:col0 + S], s2).then_inc(done, 16)
                    at += rows_

        def sp_attention(e, b, kind):
            s_ = AA if kind == "A" else BB

            def load_qk(h):
                load_parts(e, qu_s, 0, qu_d, h, False, s_["qk_loaded"])
                load_parts(e, k_s, 0, k_d, h, True, s_["qk_loaded"])

            def load_qv(h):
                load_parts(e, qv_s, 0, qv_d, h, False, qv_loaded)
                load_parts(e, pos_s, 1, pos_d, h, True, qv_loaded)

            def load_v(h):
                e.dma_start(v_s[:, :, :].rearrange("p t w -> p (t w)"),
                            v_d[bass.ds(h, 1)].rearrange("a p w -> (a p) w")).then_inc(s_["v_loaded"], 16)

            def strip_write(t, rb, db):
                k = t % RING
                for v in (e.snap(rb + (t + 1)),):
                    d = e.snap(db + 16 * (t // RING)) if t >= RING else None
                    e.wait_ge(r_free[4], v)
                    e.wait_ge(r_free[3], v)
                    if d is not None:
                        e.wait_ge(strip_in[k], d)
                    settle(e)
                e.dma_start(strip_d[k], strips[:, k * STRIP:(k + 1) * STRIP]).then_inc(strip_out[k], 16)

            def strip_read(t, T, db):
                k = t % RING
                d = e.snap(db + 16 * (t // RING + 1))
                v = e.snap(T + (t - RING + 1)) if t - 2 >= 2 else None
                e.wait_ge(strip_out[k], d)
                settle(e)
                if v is not None:
                    e.wait_ge(s_["pt_full3"], v)
                settle(e)
                skewed = bass.AP(tensor=strip_d.tensor, offset=k * P * STRIP + P - 1, ap=[[STRIP - 1, P], [1, S]])
                e.dma_start(z[:, k, :], skewed).then_inc(strip_in[k], 16)

            load_qk(0)
            load_v(0)
            if kind == "A":
                load_qv(0)
                rb = e.snap(b * (nh * NT + AHEAD))
                db = e.snap(b * (16 * (nh * 4 + 1)))
                for t in range(AHEAD):
                    strip_write(t, rb, db)
                for t in range(2):
                    strip_read(t, 0, db)
            with e.Fori(0, nh) as h:
                T = e.snap(b * (nh * NT) + h * NT)
                nxt = e.snap(h + 1)
                if kind == "A":
                    rb = e.snap(b * (nh * NT + AHEAD) + h * NT)
                    db = e.snap(b * (16 * (nh * 4 + 1)) + h * 64)
                    for s in range(NT):
                        if s == NT - AHEAD:
                            r = e.snap(rb + NT)
                            e.wait_ge(r_full[4], r)
                            settle(e)
                            load_qv(nxt)
                        strip_write(s + AHEAD, rb, db)
                        strip_read(s + 2, T, db)
                all_done = e.snap(T + NT)
                hi_done = all_done if kind == "A" else e.snap(b * (nh * 8) + h * 8 + 8)
                e.wait_ge(s_["hi_ready"], hi_done)
                settle(e)
                load_qk(nxt)
                e.wait_ge(s_["pv_done"], all_done)
                settle(e)
                load_v(nxt)
            if kind == "A":
                db = e.snap(b * (16 * (nh * 4 + 1)) + 16 * (nh * 4 + 1))
                e.wait_ge(strip_out[2], db)
                e.wait_ge(strip_out[3], db)
                for k in (2, 3):
                    skewed = bass.AP(tensor=strip_d.tensor, offset=k * P * STRIP + P - 1, ap=[[STRIP - 1, P], [1, S]])
                    e.dma_start(z[:, k, :], skewed).then_inc(strip_in[k], 16)
                for k in range(RING):
                    e.wait_ge(strip_in[k], db)
                v = e.snap(b * (QK_INC * (nh + 1)) + QK_INC * (nh + 1))
                e.wait_ge(qv_loaded, v)
                settle(e)
            v = e.snap(b * (QK_INC * (nh + 1)) + QK_INC * (nh + 1))
            e.wait_ge(s_["qk_loaded"], v)
            settle(e)
            v = e.snap(b * (16 * (nh + 1)) + 16 * (nh + 1))
            e.wait_ge(s_["v_loaded"], v)

        def oc(b, kind):
            return b * (2 * NT) + (NT if kind == "B" else 0)

        def pe_out(e, b, kind):
            w = wA if kind == "A" else wB
            base = e.snap(oc(b, kind))

            def tr(t):
                if t >= 2:
                    e.wait_ge(oo_T, base + (t - 1))
                for m in range(KT):
                    mm = e.transpose(rg[:, t % 2, m * P:(m + 1) * P], attn[:, t, m * P:(m + 1) * P], ident[:, :])
                mm.then_inc(oo_tr, 1)

            tr(0)
            for t in range(NT):
                if t + 1 < NT:
                    tr(t + 1)
                e.wait_ge(oo_T, base + (t + 1))
                if t >= 4:
                    e.wait_ge(oo_sum, base + (t - 3))
                for k in range(KT):
                    mm = e.matmul(sc[:, t % 4, 0:D], aoT[:, t % 2, k, :], w[:, 3, k, :], start=k == 0,
                                  stop=k == KT - 1)
                mm.then_inc(oo_ready, 1)

        def act_out(e, b, kind):
            base = e.snap(oc(b, kind))
            for t in range(NT):
                e.wait_ge(oo_tr, base + (t + 1))
                if t >= 2:
                    e.wait_ge(oo_ready, base + (t - 1))
                e.activation(aoT[:, t % 2, :, :], rg[:, t % 2, 0:D].rearrange("p (k c) -> p k c", k=KT),
                             ACT.Copy).then_inc(oo_T, 1)

        def dve_out(e, b, kind):
            base = e.snap(oc(b, kind))
            for t in range(NT):
                e.wait_ge(oo_ready, base + (t + 1))
                e.tensor_tensor(x_res[:, t, :], sc[:, t % 4, 0:D], x_res[:, t, :], ALU.add).then_inc(oo_sum, 1)

        def pool_out(e, b, kind):
            base = e.snap(oc(b, kind))
            for t in range(NT):
                e.wait_ge(oo_sum, base + (t + 1))
                e.tensor_tensor(x_res[:, t, :], x_res[:, t, :], rows[:, ROWS["bo" if kind == "A" else "Bbo"], :],
                                ALU.add).then_inc(oo_added, 1)

        def fc(b, k, per):
            return b * (2 * per) + k * per

        def pe_ffn(e, b, k2):
            hb = e.snap(fc(b, k2, NC * NI))
            tb = e.snap(fc(b, k2, NT))

            def up(c):
                for i in range(NI):
                    n = c * NI + i
                    if n >= 4:
                        e.wait_ge(ff_relu, hb + (n - 3))
                    for k in range(KT):
                        mm = e.matmul(sc[:, n % 4, :], w1[:, k, i * P:(i + 1) * P], xnT[:, k, c * CH:(c + 1) * CH],
                                      start=k == 0, stop=k == KT - 1)
                    mm.then_inc(ff_h, 1)

            def down(c):
                e.wait_ge(ff_relu, hb + (c + 1) * NI)
                for t in range(4 * c, 4 * c + 4):
                    if t >= 3:
                        e.wait_ge(ff_sum, tb + (t - 2))
                    for i in range(NI):
                        mm = e.matmul(rg[:, t % 3, 0:D], hT[c % 2][:, i, (t - 4 * c) * P:(t - 4 * c + 1) * P],
                                      w2[:, i, :], start=i == 0, stop=i == NI - 1)
                    mm.then_inc(ff_ready, 1)

            up(0)
            for c in range(NC):
                if c + 1 < NC:
                    up(c + 1)
                down(c)

        def act_ffn(e, b, k2):
            hb = e.snap(fc(b, k2, NC * NI))
            tb = e.snap(fc(b, k2, NT))
            for c in range(NC):
                if c >= 2:
                    e.wait_ge(ff_ready, tb + 4 * (c - 1))
                for i in range(NI):
                    n = c * NI + i
                    e.wait_ge(ff_h, hb + (n + 1))
                    e.activation(hT[c % 2][:, i, :], sc[:, n % 4, :], ACT.Relu,
                                 bias=cols[:, COLS["b1"] + i:COLS["b1"] + i + 1]).then_inc(ff_relu, 1)

        def dve_ffn(e, b, k2):
            tb = e.snap(fc(b, k2, NT))
            for t in range(NT):
                e.wait_ge(ff_ready, tb + (t + 1))
                e.tensor_tensor(x_res[:, t, :], rg[:, t % 3, 0:D], x_res[:, t, :], ALU.add).then_inc(ff_sum, 1)

        def pool_ffn(e, b, k2):
            tb = e.snap(fc(b, k2, NT))
            for t in range(NT):
                e.wait_ge(ff_sum, tb + (t + 1))
                e.tensor_tensor(x_res[:, t, :], x_res[:, t, :], rows[:, ROWS["b2"], :], ALU.add).then_inc(ff_added, 1)

        block = ctx.enter_context(nc.Block())

        @block.sync
        def _(e):
            def wload(dst, src):
                e.dma_start(dst, src).then_inc(loaded, 16)

            for i, n in enumerate(("q", "k", "v", "o")):
                wload(wA[:, i], a["A_W" + n].rearrange("(k p) n -> p k n", p=P))
                wload(wB[:, i], a["B_W" + n + "T"].rearrange("(k p) n -> p k n", p=P))
            wload(wp[:, :, :], a["A_Wp"].rearrange("(k p) n -> p k n", p=P))
            wload(w1[:, :, :], a["W1"].rearrange("(k p) n -> p k n", p=P))
            wload(w2[:, :, :], a["W2"].rearrange("(k p) n -> p k n", p=P))
            wload(cols[:, :], a["cols"])
            wload(rows[:, :, :].rearrange("p r n -> p (r n)"),
                  a["rows"].rearrange("r n -> (r n)").rearrange("(a m) -> a m", a=1).to_broadcast([P, 5 * D]))
            wload(ident[:, :], a["ident"])
            wload(sel[:, :], a["sel"])
            wload(mask[:, S - P:S], a["tri"])
            wload(embT, a["embT"].rearrange("(k p) s -> p k s", p=P))
            zd = sem_zero
            e.wait_ge(zeroed, 6)
            for d in (qu_d, qv_d, k_d, pos_d):
                e.dma_start(d[H], qu_s[0:PARTS * HD, :]).then_inc(zd, 16)
            e.dma_start(v_d[H], mask[:, 0:NT * VW]).then_inc(zd, 16)
            e.wait_ge(loaded, 16 * LOADS)
            e.wait_ge(zd, 16 * 5)
            sp_project(e, None, "pos")
            meet(e, None, 0)
            with e.Fori(0, nb) as b0:
                b = b0
                b1 = e.snap(b0 * 1)
                e.dma_start(x_res[:, :, :], a["x"][bass.ds(b0, 1)].rearrange("a (t p) n -> p (a t) n", p=P)).then_inc(
                    x_loaded, 16)
                v = e.snap(b * 16 + 16)
                e.wait_ge(x_loaded, v)
                meet_b(e, b, 1)
                meet_b(e, b, 2)
                sp_project(e, b, "A")
                sp_values(e, b, "A")
                meet_b(e, b, 3)
                sp_attention(e, b, "A")
                meet_b(e, b, 4)
                meet_b(e, b, 5)
                meet_b(e, b, 6)
                meet_b(e, b, 7)
                meet_b(e, b, 8)
                sp_project(e, b, "B")
                sp_values(e, b, "B")
                meet_b(e, b, 9)
                sp_attention(e, b, "B")
                meet_b(e, b, 10)
                meet_b(e, b, 11)
                meet_b(e, b, 12)
                meet_b(e, b, 13)
                e.dma_start(out[bass.ds(b0, 1)].rearrange("a (t p) n -> p (a t) n", p=P), x_res[:, :, :]).then_inc(
                    stored, 16)
                v = e.snap(b * 16 + 16)
                e.wait_ge(stored, v)
                settle(e)

        @block.gpsimd
        def _(e):
            e.memset(qu_s[:, :], 0.0).then_inc(zeroed, 1)
            e.memset(qv_s[:, S:S + 1], 0.0).then_inc(zeroed, 1)
            e.memset(pos_s[:, 0:1], 0.0).then_inc(zeroed, 1)
            e.memset(mask[:, 0:S - P], 0.0).then_inc(zeroed, 1)
            e.memset(mhi[:, :], 0.0).then_inc(zeroed, 1)
            e.memset(mlo[:, :], 0.0).then_inc(zeroed, 1)
            e.wait_ge(loaded, 16 * LOADS)
            pool_project(e, None, "pos")
            meet(e, None, 0)
            with e.Fori(0, nb) as b:
                meet_b(e, b, 1)
                meet_b(e, b, 2)
                pool_project(e, b, "A")
                pool_values(e, b, "A")
                meet_b(e, b, 3)
                meet_b(e, b, 4)
                pool_out(e, b, "A")
                meet_b(e, b, 5)
                meet_b(e, b, 6)
                pool_ffn(e, b, 0)
                meet_b(e, b, 7)
                meet_b(e, b, 8)
                pool_project(e, b, "B")
                pool_values(e, b, "B")
                meet_b(e, b, 9)
                meet_b(e, b, 10)
                pool_out(e, b, "B")
                meet_b(e, b, 11)
                meet_b(e, b, 12)
                pool_ffn(e, b, 1)
                meet_b(e, b, 13)

        @block.tensor
        def _(e):
            e.wait_ge(loaded, 16 * LOADS)
            pe_project(e, None, "pos", embT)
            meet(e, None, 0)
            with e.Fori(0, nb) as b:
                meet_b(e, b, 1)
                pe_norm(e, b, 0)
                meet_b(e, b, 2)
                pe_project(e, b, "A", xnT)
                pe_values(e, b, "A")
                meet_b(e, b, 3)
                pe_attention(e, b, "A")
                meet_b(e, b, 4)
                pe_out(e, b, "A")
                meet_b(e, b, 5)
                pe_norm(e, b, 1)
                meet_b(e, b, 6)
                pe_ffn(e, b, 0)
                meet_b(e, b, 7)
                pe_norm(e, b, 2)
                meet_b(e, b, 8)
                pe_project(e, b, "B", xnT)
                pe_values(e, b, "B")
                meet_b(e, b, 9)
                pe_attention(e, b, "B")
                meet_b(e, b, 10)
                pe_out(e, b, "B")
                meet_b(e, b, 11)
                pe_norm(e, b, 3)
                meet_b(e, b, 12)
                pe_ffn(e, b, 1)
                meet_b(e, b, 13)

        @block.scalar
        def _(e):
            e.wait_ge(loaded, 16 * LOADS)
            act_project(e, None, "pos")
            meet(e, None, 0)
            with e.Fori(0, nb) as b:
                meet_b(e, b, 1)
                act_norm(e, b, 0)
                meet_b(e, b, 2)
                act_project(e, b, "A")
                meet_b(e, b, 3)
                act_attention(e, b, "A")
                meet_b(e, b, 4)
                act_out(e, b, "A")
                meet_b(e, b, 5)
                act_norm(e, b, 1)
                meet_b(e, b, 6)
                act_ffn(e, b, 0)
                meet_b(e, b, 7)
                act_norm(e, b, 2)
                meet_b(e, b, 8)
                act_project(e, b, "B")
                meet_b(e, b, 9)
                act_attention(e, b, "B")
                meet_b(e, b, 10)
                act_out(e, b, "B")
                meet_b(e, b, 11)
                act_norm(e, b, 3)
                meet_b(e, b, 12)
                act_ffn(e, b, 1)
                meet_b(e, b, 13)

        @block.vector
        def _(e):
            e.wait_ge(loaded, 16 * LOADS)
            for dst, n in ((bqu, "u"), (bqv, "v")):
                e.tensor_tensor(dst[:, :], cols[:, COLS["bq"]:COLS["bq"] + KT], cols[:, COLS[n]:COLS[n] + KT],
                                ALU.add).then_inc(bias_ready, 1)
            dve_project(e, None, "pos")
            meet(e, None, 0)
            with e.Fori(0, nb) as b:
                meet_b(e, b, 1)
                dve_norm(e, b, 0)
                meet_b(e, b, 2)
                dve_project(e, b, "A")
                dve_values(e, b, "A")
                meet_b(e, b, 3)
                dve_attention(e, b, "A")
                meet_b(e, b, 4)
                dve_out(e, b, "A")
                meet_b(e, b, 5)
                dve_norm(e, b, 1)
                meet_b(e, b, 6)
                dve_ffn(e, b, 0)
                meet_b(e, b, 7)
                dve_norm(e, b, 2)
                meet_b(e, b, 8)
                dve_project(e, b, "B")
                dve_values(e, b, "B")
                meet_b(e, b, 9)
                dve_attention(e, b, "B")
                meet_b(e, b, 10)
                dve_out(e, b, "B")
                meet_b(e, b, 11)
                dve_norm(e, b, 3)
                meet_b(e, b, 12)
                dve_ffn(e, b, 1)
                meet_b(e, b, 13)


def constants():
    pos = np.arange(S, dtype=np.float32)
    idx = np.arange(D // 2, dtype=np.float32)
    inv_freq = np.float32(1.0) / np.float32(10000.0) ** (np.float32(2.0) * idx / np.float32(D))
    ang = pos[:, None] * inv_freq[None, :].astype(np.float32)
    emb = np.concatenate([np.sin(ang), np.cos(ang)], axis=-1).astype(np.float32)
    sel = np.zeros((P, VW), np.float32)
    for p in range(P):
        sel[p, p % VW] = 1.0
    tri = np.where(np.arange(P)[None, :] > np.arange(P)[:, None], NEG, 0.0).astype(np.float32)
    return {"embT": np.ascontiguousarray(emb.T), "ident": np.eye(P, dtype=np.float32), "sel": sel, "tri": tri}


def arrays_of(i):
    c = np.ascontiguousarray

    def two(x):
        return np.asarray(x).reshape(-1, P).T

    arr = {"x": c(i["L0_attn_a_x"])}
    for n in "qkvpo":
        arr["A_W" + n] = c(i["L0_attn_a_W" + n])
    for n in "qkvo":
        arr["B_W" + n + "T"] = c(np.asarray(i["L0_attn_b_W" + n]).T)
    arr["W1"] = c(i["L0_ffn_W1"])
    arr["W2"] = c(i["L0_ffn_W2"])
    arr["cols"] = c(np.concatenate([two(i[n]) for n in (
        "L0_attn_a_bq", "L0_attn_a_bk", "L0_attn_a_bp", "L0_attn_a_u", "L0_attn_a_v", "L0_attn_b_bq",
        "L0_attn_b_bk", "L0_ffn_b1")], axis=1))
    arr["rows"] = c(np.stack([np.asarray(i[n]) for n in (
        "L0_attn_a_bv", "L0_attn_a_bo", "L0_attn_b_bv", "L0_attn_b_bo", "L0_ffn_b2")]))
    arr.update(constants())
    return arr


def kernel(**inputs):
    import concourse.bacc as bacc
    from concourse.bass_utils import run_bass_kernel_spmd

    nc = bacc.Bacc("TRN2", target_bir_lowering=False, num_devices=1)
    arrays = {"in_" + n: v for n, v in arrays_of(inputs).items()}
    aps = {n[3:]: nc.dram_tensor(n, v.shape, mybir.dt.from_np(v.dtype), kind="ExternalInput").ap()
           for n, v in arrays.items()}
    shape = inputs["L0_attn_a_x"].shape
    out = nc.dram_tensor("out_0_dram", shape, F32, kind="ExternalOutput").ap()
    program(nc, aps, out)
    r = run_bass_kernel_spmd(nc, [arrays], core_ids=[0])
    return r.results[0]["out_0_dram"]
```

```python
from contextlib import ExitStack

import numpy as np

import concourse.bass as bass
from concourse import mybir

F32 = mybir.dt.float32
BF16 = mybir.dt.bfloat16
ALU = mybir.AluOpType
ACT = mybir.ActivationFunctionType
AX = mybir.AxisListType

P = 128
D = 256
KT = D // P
H = 16
HD = D // H
S = 2048
NT = S // P
CH = 512
NC = S // CH
INTER = 1024
NI = INTER // P
PARTS = 3
SLOTS = 6
KROWS = SLOTS * HD
STRIP = S + P
RING = 4
AHEAD = 4
VW = 32
SCALE = 1.0 / float(np.sqrt(HD))
EPS = 1e-5
NEG = -1.0e30

R_CHUNKS = [(c * CH, min(CH, STRIP - c * CH)) for c in range(5)]
R_BANK = [0, 1, 2, 0, 1]
R_BY_DVE = [3]
P_BANK = [2, 0, 1, 2]
P_BY_DVE = [0, 1]
HB = 4
NB = 2
G = HB * NT
LAG = dict(A=1, B=2)
OB = 4
B_BANK = [0, 1, 2, 0]

COLS = dict(bq=0, bk=2, bp=4, u=6, v=8, Bbq=10, Bbk=12, b1=14)
NCOLS = 22
ROWS = dict(bv=0, bo=1, Bbv=2, Bbo=3, b2=4)


def program(nc, a, out, nb=4, nh=H):
    ctx = ExitStack()
    with ctx:
        def sb(name, shape, dt=F32):
            return ctx.enter_context(nc.sbuf_tensor(name, shape, dt))

        def pb(name, shape):
            return ctx.enter_context(nc.psum_tensor(name, shape, F32))

        def sem(name):
            return ctx.enter_context(nc.semaphore(name))

        qu_d = nc.dram_tensor("qu_parts", (H + NB, PARTS * HD, S), BF16).ap()
        qv_d = nc.dram_tensor("qv_parts", (H + NB, PARTS * HD, S), BF16).ap()
        k_d = nc.dram_tensor("k_parts", (H + NB, PARTS * HD, S), BF16).ap()
        pos_d = nc.dram_tensor("pos_parts", (H + NB, PARTS * HD, S), BF16).ap()
        v_d = nc.dram_tensor("v_heads", (H + NB, P, NT * VW), F32).ap()
        strip_d = nc.dram_tensor("strips", (RING, P, STRIP), F32).ap()

        x_res = sb("x_res", [P, NT, D])
        xnT = sb("xnT", [P, KT, S])
        attn = sb("attn", [P, NT, D])
        qv_s = [sb("qv_s0", [KROWS, S + 1], BF16), sb("qv_s1", [KROWS, S + 1], BF16)]
        pos_s = [sb("pos_s0", [KROWS, S + 1], BF16), sb("pos_s1", [KROWS, S + 1], BF16)]
        k_sb = sb("k_sb", [KROWS, S], BF16)
        strips = sb("strips_sb", [P, RING * STRIP])
        z = sb("z", [P, RING, S])
        pT = sb("pT", [P, 2, S])
        po_sb = sb("po_sb", [P, OB, P])
        rsum = sb("rsum", [P, OB])
        mlo = sb("mlo", [P, 2])
        mhi = sb("mhi", [P, 2])
        nmax = sb("nmax", [P, 2])
        idle = sb("idle", [P, 1])
        wA = sb("wA", [P, 4, KT, D])
        wB = sb("wB", [P, 4, KT, D])
        wp = sb("wp", [P, KT, D])
        w1 = sb("w1", [P, KT, INTER])
        w2 = sb("w2", [P, NI, D])
        cols = sb("cols", [P, NCOLS])
        rows = sb("rows", [P, 5, D])
        ident = sb("ident", [P, P])
        sel = sb("sel", [P, VW])
        mask = sb("mask", [P, S])
        bqu = sb("bqu", [P, KT])
        bqv = sb("bqv", [P, KT])
        stats = sb("stats", [P, NT, 6])
        mv = sb("mv", [P, NT, 2])
        ve = sb("ve", [P, NT])
        rstd = sb("rstd", [P, NT])
        nwt = sb("nwt", [P, 3, NT])
        xn = sb("xn", [P, 2, D])
        aoT = sb("aoT", [P, 2, KT, P])

        xnT_f = xnT[:, :, :].rearrange("p k s -> p (k s)")
        qk2 = xnT_f[0:KROWS, 0:S].bitcast(BF16)
        v_at = [S + i * NT * VW for i in range(NB)]
        qu_at = S + NB * NT * VW
        qu_s = [xnT_f[0:KROWS, qu_at:qu_at + S // 2].bitcast(BF16), qk2[:, 0:S]]
        k_s = [k_sb[:, :], qk2[:, S:2 * S]]
        v_s = [xnT_f[:, at:at + NT * VW].rearrange("p (t w) -> p t w", t=NT) for at in v_at]

        zf = z[:, :, :].rearrange("p r s -> p (r s)")
        zb = zf.bitcast(BF16)
        parts = [[zb[:, (2 * 3 + 0) * 0 + (s * 3 + i) * S:(s * 3 + i + 1) * S] for i in range(PARTS)] for s in range(2)]
        resid = [zf[:, 3 * S + i * CH:3 * S + (i + 1) * CH] for i in range(4)]
        v_all = strips[:, 0:H * NT * VW].rearrange("p (h t w) -> p h t w", h=H, t=NT)
        hT = [strips[:, i * NI * CH:(i + 1) * NI * CH].rearrange("p (n c) -> p n c", n=NI) for i in range(2)]
        embT = strips[:, 0:KT * S].rearrange("p (k s) -> p k s", k=KT)

        sc = pb("sc", [P, 4, CH])
        rg = pb("rg", [P, 3, CH])
        op = pb("op", [P, CH])
        po = op[:, 0:P]
        on = op[:, P:P + OB * VW].rearrange("p (o w) -> p o w", o=OB)
        scf = sc[:, :, :].rearrange("p b c -> p (b c)")

        phase_done = sem("phase_done")
        waited = sem("waited")
        loaded = sem("loaded")
        zeroed = sem("zeroed")
        bias_ready = sem("bias_ready")
        x_loaded = sem("x_loaded")
        stored = sem("stored")
        ln_stat = sem("ln_stat")
        ln_var = sem("ln_var")
        ln_sqrt = sem("ln_sqrt")
        ln_step = sem("ln_step")
        ln_xn = sem("ln_xn")
        ln_tr = sem("ln_tr")
        ln_out = sem("ln_out")
        pj_ready = sem("pj_ready")
        pj_high = sem("pj_high")
        pj_resid = sem("pj_resid")
        pj_mid = sem("pj_mid")
        pj_low = sem("pj_low")
        pj_stored = [sem("pj_stored0"), sem("pj_stored1")]
        pv_ready = sem("pv_ready")
        pv_added = sem("pv_added")
        pv_pad = sem("pv_pad")
        pv_stored = sem("pv_stored")
        oo_tr = sem("oo_tr")
        oo_T = sem("oo_T")
        oo_ready = sem("oo_ready")
        oo_sum = sem("oo_sum")
        oo_added = sem("oo_added")
        ff_h = sem("ff_h")
        ff_relu = sem("ff_relu")
        ff_ready = sem("ff_ready")
        ff_sum = sem("ff_sum")
        ff_added = sem("ff_added")
        names = ["lo_ready", "hi_ready", "lo_read", "hi_read", "maxes", "nmax_ready", "exp_done", "pv_done",
                 "po_copied", "comb_done", "rcp", "out_read", "qk_loaded0", "qk_loaded1", "v_loaded0", "v_loaded1"]
        AA = {n: sem("A_" + n) for n in names}
        BB = {n: sem("B_" + n) for n in names}
        for q in range(4):
            AA[f"pt_full{q}"] = sem(f"A_pt_full{q}")
            AA[f"pt_free{q}"] = sem(f"A_pt_free{q}")
        for n in ("pt_by_act", "pt_by_dve"):
            BB[n] = sem("B_" + n)
        r_full = [sem(f"r_full{c}") for c in range(5)]
        r_free = [sem(f"r_free{c}") for c in range(5)]
        strip_out = [sem(f"strip_out{k}") for k in range(RING)]
        strip_in = [sem(f"strip_in{k}") for k in range(RING)]
        qv_loaded = [sem("qv_loaded0"), sem("qv_loaded1")]
        sem_zero = sem("spare_head_zero")

        NPH = 12
        ENG = 5
        LOADS = 17
        QK_INC = 16 * (3 + 6)

        def meet(e, b, k):
            e.drain().then_inc(phase_done, 1)
            e.wait_ge(phase_done, ENG)

        def settle(e):
            e.sem_inc(waited, 1)

        def meet_b(e, b, k):
            v = e.snap(b * (ENG * 13) + ENG * (k + 1))
            settle(e)
            e.drain().then_inc(phase_done, 1)
            e.wait_ge(phase_done, v)
            settle(e)

        def jobs(kind):
            if kind == "pos":
                return [(wp[:, :, :], cols[:, COLS["bp"] + m:COLS["bp"] + m + 1], pos_d, m) for m in range(KT)]
            if kind == "A":
                return ([(wA[:, 0], bqu[:, m:m + 1], qu_d, m) for m in range(KT)]
                        + [(wA[:, 0], bqv[:, m:m + 1], qv_d, m) for m in range(KT)]
                        + [(wA[:, 1], cols[:, COLS["bk"] + m:COLS["bk"] + m + 1], k_d, m) for m in range(KT)])
            return ([(wB[:, 0], cols[:, COLS["Bbq"] + m:COLS["Bbq"] + m + 1], qu_d, m) for m in range(KT)]
                    + [(wB[:, 1], cols[:, COLS["Bbk"] + m:COLS["Bbk"] + m + 1], k_d, m) for m in range(KT)])

        NJ = {"pos": 2, "A": 6, "B": 4}
        JB = NJ["A"] + NJ["B"]
        JOFF = {"pos": 0, "A": NJ["pos"], "B": NJ["pos"] + NJ["A"]}

        def jbase(b, kind):
            return JOFF[kind] if kind == "pos" else b * JB + JOFF[kind]

        def times(x, k):
            return x * k

        def pe_project(e, b, kind, src):
            jb = jbase(b, kind)
            for j, (w, _, _, m) in enumerate(jobs(kind)):
                for c in range(NC):
                    n = j * NC + c
                    if kind == "pos" and n < 4:
                        pass
                    else:
                        if n >= 4:
                            e.wait_ge(pj_resid, jb * NC + (n - 3))
                    for k in range(KT):
                        mm = e.matmul(sc[:, c, :], w[:, k, m * P:(m + 1) * P], src[:, k, c * CH:(c + 1) * CH],
                                      start=k == 0, stop=k == KT - 1)
                    mm.then_inc(pj_ready, 1)

        def act_project(e, b, kind):
            jb = jbase(b, kind)
            for j, (_, bias, _, m) in enumerate(jobs(kind)):
                if j >= 2:
                    e.wait_ge(pj_stored[j % 2], pj_count(b, kind, j - 2))
                for c in range(NC):
                    n = j * NC + c
                    e.wait_ge(pj_ready, jb * NC + (n + 1))
                    e.activation(parts[j % 2][0][:, c * CH:(c + 1) * CH], sc[:, c, :], ACT.Identity,
                                 bias=bias).then_inc(pj_high, 1)

        def dve_project(e, b, kind):
            jb = jbase(b, kind)
            for j, (_, bias, _, m) in enumerate(jobs(kind)):
                for c in range(NC):
                    n = j * NC + c
                    e.wait_ge(pj_high, jb * NC + (n + 1))
                    if n >= 4:
                        e.wait_ge(pj_low, jb * NC + (n - 3))
                    e.scalar_tensor_tensor(out=resid[c], in0=sc[:, c, :], scalar=bias,
                                           in1=parts[j % 2][0][:, c * CH:(c + 1) * CH],
                                           op0=ALU.add, op1=ALU.subtract).then_inc(pj_resid, 1)

        def pool_project(e, b, kind):
            jb = jbase(b, kind)
            for j in range(NJ[kind]):
                if j >= 2:
                    e.wait_ge(pj_stored[j % 2], pj_count(b, kind, j - 2))
                for c in range(NC):
                    n = j * NC + c
                    cs = slice(c * CH, (c + 1) * CH)
                    e.wait_ge(pj_resid, jb * NC + (n + 1))
                    settle(e)
                    e.tensor_copy(parts[j % 2][1][:, cs], resid[c]).then_inc(pj_mid, 1)
                    e.wait_ge(pj_mid, jb * NC + (n + 1))
                    e.tensor_tensor(parts[j % 2][2][:, cs], resid[c], parts[j % 2][1][:, cs],
                                    ALU.subtract).then_inc(pj_low, 1)

        def pj_count(b, kind, j):
            js = (j // 2 + 1)
            off = JOFF[kind] // 2
            per = 16 * PARTS
            return per * (off + js) if kind == "pos" else b * (per * (JB // 2)) + per * (off + js)

        def sp_project(e, b, kind):
            jb = jbase(b, kind)
            for j, (_, _, dst, m) in enumerate(jobs(kind)):
                e.wait_ge(pj_low, jb * NC + (j + 1) * NC)
                settle(e)
                hs = dst[m * (H // KT):(m + 1) * (H // KT), :, :].rearrange("h (a d) s -> a h d s", a=PARTS)
                for i in range(PARTS):
                    e.dma_start(hs[i], parts[j % 2][i]).then_inc(pj_stored[j % 2], 16)
            for j in (NJ[kind] - 2, NJ[kind] - 1):
                e.wait_ge(pj_stored[j % 2], pj_count(b, kind, j))
                settle(e)

        def vcount(b, kind, per):
            return b * (2 * per) + (per if kind == "B" else 0)

        def pe_values(e, b, kind):
            w = wA if kind == "A" else wB
            base = vcount(b, kind, NT)
            for t in range(NT):
                if t >= 3:
                    e.wait_ge(pv_added, base + (t - 2))
                for k in range(KT):
                    mm = e.matmul(rg[:, t % 3, 0:D], xnT[:, k, t * P:(t + 1) * P], w[:, 2, k, :],
                                  start=k == 0, stop=k == KT - 1)
                mm.then_inc(pv_ready, 1)

        def dve_values(e, b, kind):
            bv = rows[:, ROWS["bv" if kind == "A" else "Bbv"], :].rearrange("p (h d) -> p h d", h=H)
            base = vcount(b, kind, NT)
            for t in range(NT):
                e.wait_ge(pv_ready, base + (t + 1))
                e.tensor_tensor(v_all[:, :, t, 0:HD], rg[:, t % 3, 0:D].rearrange("p (h d) -> p h d", h=H), bv,
                                ALU.add).then_inc(pv_added, 1)

        def pool_values(e, b, kind):
            e.memset(v_all[:, :, :, HD + 1:VW], 0.0).then_inc(pv_pad, 1)
            e.memset(v_all[:, :, :, HD:HD + 1], 1.0).then_inc(pv_pad, 1)

        def sp_values(e, b, kind):
            e.wait_ge(pv_added, vcount(b, kind, NT) + NT)
            settle(e)
            e.wait_ge(pv_pad, vcount(b, kind, 2) + 2)
            e.dma_start(v_d[0:H].rearrange("h p w -> p h w"),
                        strips[:, 0:H * NT * VW].rearrange("p (h w) -> p h w", h=H)).then_inc(pv_stored, 16)
            e.wait_ge(pv_stored, vcount(b, kind, 16) + 16)

        def lc(b, k, per):
            return b * (4 * per) + k * per

        def dve_norm(e, b, k):
            for t in range(NT):
                e.bn_stats(stats[:, t, :], x_res[:, t, :]).then_inc(ln_stat, 1)
            for t in range(NT):
                e.wait_ge(ln_stat, lc(b, k, NT) + (t + 1))
                settle(e)
                e.bn_aggr(mv[:, t, :], stats[:, t, :]).then_inc(ln_var, 1)
            e.wait_ge(ln_var, lc(b, k, NT) + NT)
            base = lc(b, k, 6)
            e.tensor_scalar(ve[:, :], mv[:, :, 1], EPS, None, ALU.add).then_inc(ln_step, 1)
            e.wait_ge(ln_sqrt, lc(b, k, 1) + 1)
            e.reciprocal(nwt[:, 1, :], nwt[:, 0, :]).then_inc(ln_step, 1)
            e.wait_ge(ln_step, base + 2)
            e.tensor_tensor(nwt[:, 2, :], nwt[:, 1, :], nwt[:, 1, :], ALU.mult).then_inc(ln_step, 1)
            e.wait_ge(ln_step, base + 3)
            e.tensor_tensor(nwt[:, 2, :], nwt[:, 2, :], ve[:, :], ALU.mult).then_inc(ln_step, 1)
            e.wait_ge(ln_step, base + 4)
            e.tensor_scalar(nwt[:, 2, :], nwt[:, 2, :], -0.5, 1.5, ALU.mult, ALU.add).then_inc(ln_step, 1)
            e.wait_ge(ln_step, base + 5)
            e.tensor_tensor(rstd[:, :], nwt[:, 2, :], nwt[:, 1, :], ALU.mult).then_inc(ln_step, 1)
            e.wait_ge(ln_step, base + 6)
            for t in range(NT):
                if t >= 2:
                    e.wait_ge(ln_tr, lc(b, k, NT) + (t - 1))
                e.tensor_scalar(xn[:, t % 2, :], x_res[:, t, :], mv[:, t, 0:1], rstd[:, t:t + 1],
                                ALU.subtract, ALU.mult).then_inc(ln_xn, 1)

        def act_norm(e, b, k):
            e.wait_ge(ln_step, lc(b, k, 6) + 1)
            e.activation(nwt[:, 0, :], ve[:, :], ACT.Sqrt).then_inc(ln_sqrt, 1)
            for t in range(NT):
                e.wait_ge(ln_tr, lc(b, k, NT) + (t + 1))
                e.activation(xnT[:, :, t * P:(t + 1) * P], rg[:, t % 3, 0:D].rearrange("p (k c) -> p k c", k=KT),
                             ACT.Copy).then_inc(ln_out, 1)

        def pe_norm(e, b, k):
            for t in range(NT):
                e.wait_ge(ln_xn, lc(b, k, NT) + (t + 1))
                if t >= 3:
                    e.wait_ge(ln_out, lc(b, k, NT) + (t - 2))
                for m in range(KT):
                    mm = e.transpose(rg[:, t % 3, m * P:(m + 1) * P], xn[:, t % 2, m * P:(m + 1) * P], ident[:, :])
                mm.then_inc(ln_tr, 1)

        def loads_of(k):
            return nh // NB + (1 if k == 0 else 0)

        def load_count(b, p, hd, inc):
            return b * (inc * loads_of(hd % NB)) + p * (HB // NB * inc) + (hd // NB + 1) * inc

        def pe_attention(e, b, kind):
            s_ = AA if kind == "A" else BB
            lag = LAG[kind]

            def strip(t, rb, qv_at, chunks=range(5)):
                hd = t // NT % NB
                i0 = (t % NT) * P
                edge = i0 + P
                if t % NT == 0 and 0 in chunks:
                    e.wait_ge(qv_loaded[hd], qv_at + QK_INC * (t // NT // NB))
                for c in chunks:
                    c0, w = R_CHUNKS[c]
                    bank = R_BANK[c]
                    claim(bank)
                    for lo, hi, first in ((c0, min(c0 + w, edge), True), (max(c0, edge), c0 + w, False)):
                        if lo >= hi:
                            continue
                        if first:
                            q = qv_s[hd][:, i0:i0 + P]
                            m0 = 1 + S - P - i0 + lo
                        else:
                            q = qv_s[hd][:, i0 + 1:i0 + P + 1]
                            m0 = lo - edge
                        mm = e.matmul(rg[:, bank, lo - c0:hi - c0], q, pos_s[hd][:, m0:m0 + hi - lo],
                                      start=True, stop=True)
                    mm.then_inc(r_full[c], 1)
                    last[bank] = (r_free[c], rb + (t + 1))

            last = {}

            def claim(bank):
                if bank in last:
                    e.wait_ge(*last.pop(bank))

            if kind == "A":
                rb = e.snap(b * (nh * NT + AHEAD))
                for t in range(AHEAD):
                    strip(t, rb, b * (QK_INC * (nh // NB + 1)) + QK_INC)
                for bank in range(3):
                    claim(bank)
                settle(e)

            def content(g):
                s, hd = g % NT, g // NT
                if s == 0:
                    e.wait_ge(s_[f"qk_loaded{hd % NB}"], load_count(b, p, hd, QK_INC))
                width = S if kind == "A" else (s + 1) * P
                for half, ready, read in ((0, "lo_ready", "lo_read"), (1, "hi_ready", "hi_read")):
                    c0s = [c for c in (2 * half, 2 * half + 1) if c * CH < width]
                    if not c0s:
                        continue
                    if g >= 1:
                        n = halves_before(kind, g, half)
                        if n:
                            e.wait_ge(s_[read], hbase(kind, T, b, p, half) + n)
                    for c in c0s:
                        w = min(CH, width - c * CH)
                        mm = e.matmul(sc[:, c, 0:w], qu_s[hd % NB][:, s * P:(s + 1) * P], k_s[hd % NB][:, c * CH:c * CH + w],
                                      start=True, stop=True)
                    mm.then_inc(s_[ready], 1)

            def combine(t):
                ng = 4 if kind == "A" else min(4, t % NT + 1)
                e.wait_ge(s_["po_copied"], T + (t + 1))
                mm = e.matmul(on[:, t % OB, :], po_sb[0:32 * ng, t % OB, :], sel[0:32 * ng, :], start=True, stop=True)
                if t % OB == OB - 1:
                    mm.then_inc(s_["comb_done"], 1)

            with e.Fori(0, nh // HB) as p:
                T = e.snap(b * (nh * NT) + p * G)
                U = e.snap(b * (nh * NT // OB) + p * (G // OB))
                last.clear()
                if kind == "A":
                    rb = e.snap(b * (nh * NT + AHEAD) + p * G)
                    ql = e.snap(b * (QK_INC * (nh // NB + 1)) + p * (HB // NB * QK_INC) + QK_INC)
                content(0)
                for s in range(G + lag + 1):
                    if kind == "A" and s < G:
                        strip(s + AHEAD, rb, ql, (0, 1))
                    if s > lag and (s - lag - 1) % NT == 0:
                        hd = (s - lag - 1) // NT
                        e.wait_ge(s_[f"v_loaded{hd % NB}"], load_count(b, p, hd, 16))
                    if s > lag:
                        t = s - lag - 1
                        if t % OB:
                            combine(t - 1)
                        elif t >= OB:
                            e.wait_ge(s_["out_read"], U + t // OB)
                        if kind == "A":
                            e.wait_ge(s_["pt_free1"], T + (t + 1))
                            e.wait_ge(s_["pt_free3"], T + (t + 1))
                        else:
                            e.wait_ge(s_["pt_by_act"], T + (t + 1))
                            e.wait_ge(s_["pt_by_dve"], T + (t + 1))
                        nj = NT if kind == "A" else t % NT + 1
                        nj4 = max(nj, 4) if kind == "A" else nj
                        for j in range(nj4):
                            g = j % 4
                            mm = e.matmul(po[32 * g:32 * g + 32, :], v_s[t // NT % NB][:, j, :], pT[:, t % 2, j * P:(j + 1) * P],
                                          start=j < 4, stop=j + 4 >= nj)
                        mm.then_inc(s_["pv_done"], 1)
                    if kind == "A":
                        if s < G:
                            strip(s + AHEAD, rb, ql, (2,))
                        if s + 1 < G:
                            content(s + 1)
                        if s > lag and (s - lag) % OB == 0:
                            combine(s - lag - 1)
                        if s < G:
                            strip(s + AHEAD, rb, ql, (3, 4))
                    if lag <= s < G + lag:
                        t = s - lag
                        e.wait_ge(s_["exp_done"], T + (t + 1))
                        nblk = NT if kind == "A" else t % NT + 1
                        if kind == "B" and t >= 1:
                            e.wait_ge(s_["pt_by_act"], T + t)
                            e.wait_ge(s_["pt_by_dve"], T + t)
                        for q in range(4):
                            blks = range(4 * q, min(4 * q + 4, nblk))
                            if not len(blks):
                                continue
                            if kind == "A":
                                bank = P_BANK[q]
                                claim(bank)
                            else:
                                bank = B_BANK[q]
                                if q == 3:
                                    e.wait_ge(pt_first, b * (nh * 4) + p * (HB * 4) + four_chunk(t))
                            for j in blks:
                                mm = e.transpose(rg[:, bank, (j - 4 * q) * P:(j - 4 * q + 1) * P],
                                                 z[:, t % RING, j * P:(j + 1) * P], ident[:, :])
                            if kind == "A":
                                mm.then_inc(s_[f"pt_full{q}"], 1)
                                last[bank] = (s_[f"pt_free{q}"], T + (t + 1))
                            else:
                                mm.then_inc(b_full[q], 1)
                    if kind == "B":
                        if s > lag and (s - lag) % OB == 0:
                            combine(s - lag - 1)
                        if s + 1 < G:
                            content(s + 1)

        pt_first = sem("B_pt_first")
        b_full = [sem(f"B_pt_full{q}") for q in range(4)]

        def chunk_base(b, p, q):
            return b * (nh * (NT - 4 * q)) + p * (HB * (NT - 4 * q))

        def chunk_count(t, q):
            return t // NT * (NT - 4 * q) + t % NT - 4 * q + 1

        def wait_chunk(e, b, p, t, q):
            e.wait_ge(b_full[q], chunk_base(b, p, q) + chunk_count(t, q))

        def halves_before(kind, g, half):
            if kind == "A" or half == 0:
                return g
            return g // NT * (NT // 2) + max(0, g % NT - NT // 2)

        def hbase(kind, T, b, p, half):
            if kind == "A" or half == 0:
                return T
            return b * (nh * (NT // 2)) + p * (HB * (NT // 2))

        def four_chunk(t):
            return t // NT * 4 + t % NT - 11

        def move_strip(e, op_copy, c, t, rb, wb):
            c0, w = R_CHUNKS[c]
            e.wait_ge(r_full[c], rb + (t + 1))
            if t >= RING and (c == 3 or c == 0):
                e.wait_ge(strip_out[t % RING], wb + 16 * (t // RING))
            k = t % RING
            op_copy(strips[:, k * STRIP + c0:k * STRIP + c0 + w], rg[:, R_BANK[c], 0:w]).then_inc(r_free[c], 1)

        def act_copy(e):
            return lambda o, i: e.activation(o, i, ACT.Copy)

        def act_attention(e, b, kind):
            s_ = AA if kind == "A" else BB
            lag = LAG[kind]
            if kind == "A":
                rb = e.snap(b * (nh * NT + AHEAD))
                for t in range(AHEAD):
                    for c in range(5):
                        if c not in R_BY_DVE:
                            move_strip(e, act_copy(e), c, t, rb, 0)
            with e.Fori(0, nh // HB) as p:
                T = e.snap(b * (nh * NT) + p * G)
                if kind == "A":
                    rb = e.snap(b * (nh * NT + AHEAD) + p * G)
                    wb = e.snap(b * (16 * (nh * 4 + 1)) + p * (16 * G // RING))
                for s in range(G + lag):
                    if kind == "A" and s < G:
                        for c in range(5):
                            if c not in R_BY_DVE:
                                move_strip(e, act_copy(e), c, s + AHEAD, rb, wb)
                    if kind == "A" and s < G:
                        w = S
                        e.wait_ge(s_["nmax_ready"], T + (s + 1))
                        e.activation(z[:, s % RING, 0:w], z[:, s % RING, 0:w], ACT.Exp,
                                     bias=nmax[:, s % 2:s % 2 + 1], scale=SCALE).then_inc(s_["exp_done"], 1)
                    if lag <= s:
                        t = s - lag
                        if t >= 2:
                            e.wait_ge(s_["pv_done"], T + (t - 1))
                        if kind == "A":
                            for q in range(4):
                                if q in P_BY_DVE:
                                    continue
                                e.wait_ge(s_[f"pt_full{q}"], T + (t + 1))
                                e.activation(pT[:, t % 2, q * CH:(q + 1) * CH], rg[:, P_BANK[q], :],
                                             ACT.Copy).then_inc(s_[f"pt_free{q}"], 1)
                        else:
                            nblk = t % NT + 1
                            for q in (0, 1, 3):
                                if nblk <= 4 * q or (q == 1 and nblk <= 8):
                                    continue
                                wait_chunk(e, b, p, t, q)
                                w = min(CH, nblk * P - q * CH)
                                mm = e.activation(pT[:, t % 2, q * CH:q * CH + w], rg[:, B_BANK[q], 0:w], ACT.Copy)
                                if q == 0 and nblk > 12:
                                    mm.then_inc(pt_first, 1)
                                    mm = None
                            mm.then_inc(s_["pt_by_act"], 1)
                    if kind == "B" and s < G:
                        w = (s % NT + 1) * P
                        e.wait_ge(s_["nmax_ready"], T + (s + 1))
                        e.activation(z[:, s % RING, 0:w], z[:, s % RING, 0:w], ACT.Exp,
                                     bias=nmax[:, s % 2:s % 2 + 1], scale=SCALE).then_inc(s_["exp_done"], 1)

        def maximum(e, kind, b, p, T, s):
            s_ = AA if kind == "A" else BB
            lo, hi, nm = mlo[:, s % 2:s % 2 + 1], mhi[:, s % 2:s % 2 + 1], nmax[:, s % 2:s % 2 + 1]
            e.wait_ge(s_["lo_read"], T + (s + 1))
            if s >= 2:
                e.wait_ge(s_["exp_done"], T + (s - 1))
            if kind == "A" or s % NT * P >= 2 * CH:
                e.wait_ge(s_["hi_read"], hbase(kind, T, b, p, 1) + (halves_before(kind, s, 1) + 1))
                if kind == "B":
                    settle(e)
                e.tensor_scalar(nm, lo, hi, -SCALE, ALU.max, ALU.mult).then_inc(s_["nmax_ready"], 1)
            else:
                if kind == "B":
                    settle(e)
                e.tensor_scalar(nm, lo, -SCALE, None, ALU.mult).then_inc(s_["nmax_ready"], 1)

        def pool_attention(e, b, kind):
            with e.Fori(0, nh // HB) as p:
                T = e.snap(b * (nh * NT) + p * G)
                for s in range(G):
                    maximum(e, kind, b, p, T, s)

        def dve_attention(e, b, kind):
            s_ = AA if kind == "A" else BB
            lag = LAG[kind]
            if kind == "A":
                rb = e.snap(b * (nh * NT + AHEAD))
                for t in range(AHEAD):
                    move_strip(e, e.tensor_copy, 3, t, rb, 0)
            def normalise(t):
                if t % OB != OB - 1:
                    return
                e.wait_ge(s_["comb_done"], U + (t // OB + 1))
                e.reciprocal(rsum[:, :], on[:, :, HD]).then_inc(s_["rcp"], 1)
                e.wait_ge(s_["rcp"], U + (t // OB + 1))
                t0 = t % NT - OB + 1
                e.tensor_tensor(attn[:, t0:t0 + OB, bass.ds(p * (HB * HD) + t // NT * HD, HD)], on[:, :, 0:HD],
                                rsum[:, :].rearrange("p (o w) -> p o w", w=1).to_broadcast([P, OB, HD]),
                                ALU.mult).then_inc(s_["out_read"], 1)

            with e.Fori(0, nh // HB) as p:
                T = e.snap(b * (nh * NT) + p * G)
                U = e.snap(b * (nh * NT // OB) + p * (G // OB))
                if kind == "A":
                    rb = e.snap(b * (nh * NT + AHEAD) + p * G)
                    wb = e.snap(b * (16 * (nh * 4 + 1)) + p * (16 * G // RING))
                    lb = e.snap(b * (16 * (nh * 4 + 1)) + p * (16 * G // RING))
                for s in range(G + lag + 1):
                    if s < G:
                        width = S if kind == "A" else (s % NT + 1) * P
                        if kind == "A":
                            e.wait_ge(strip_in[s % RING], lb + 16 * (s // RING + 1))
                        elif s >= RING:
                            wait_chunk(e, b, p, s - RING, (s - RING) % NT // 4)
                        lo, hi = mlo[:, s % 2:s % 2 + 1], mhi[:, s % 2:s % 2 + 1]
                        if s >= 2:
                            e.wait_ge(s_["nmax_ready"], T + (s - 1))
                        halves = [(0, "lo_ready", "lo_read", lo), (1, "hi_ready", "hi_read", hi)]
                        halves = [x for x in halves if x[0] * 2 * CH < width]
                        for half, ready, read, mx in halves:
                            c0 = half * 2 * CH
                            c1 = min(width, c0 + 2 * CH)
                            e.wait_ge(s_[ready], hbase(kind, T, b, p, half) + (halves_before(kind, s, half) + 1))
                            settle(e)
                            zs = z[:, s % RING, c0:c1]
                            add = zs if kind == "A" else mask[:, S - width + c0:S - width + c1]
                            e.tensor_tensor_reduce(out=zs, in0=scf[:, c0:c1], in1=add, scale=1.0, scalar=-3.0e38,
                                                   op0=ALU.add, op1=ALU.max, accum_out=mx).then_inc(s_[read], 1)
                        if kind == "A":
                            maximum(e, kind, b, p, T, s)
                    if s > lag:
                        t = s - lag - 1
                        ng = 4 if kind == "A" else min(4, t % NT + 1)
                        e.wait_ge(s_["pv_done"], T + (t + 1))
                        e.tensor_copy(po_sb[0:32 * ng, t % OB, :], po[0:32 * ng, :]).then_inc(s_["po_copied"], 1)
                    if kind == "A" and s < G:
                        move_strip(e, e.tensor_copy, 3, s + AHEAD, rb, wb)
                    if lag <= s < G + lag:
                        t = s - lag
                        if t >= 2:
                            e.wait_ge(s_["pv_done"], T + (t - 1))
                        if kind == "A":
                            for q in P_BY_DVE:
                                e.wait_ge(s_[f"pt_full{q}"], T + (t + 1))
                                e.tensor_copy(pT[:, t % 2, q * CH:(q + 1) * CH],
                                              rg[:, P_BANK[q], :]).then_inc(s_[f"pt_free{q}"], 1)
                        else:
                            nblk = t % NT + 1
                            q = 2 if nblk > 8 else 1
                            c0 = q * CH
                            w = min(nblk * P, 3 * CH) - c0
                            if w > 0:
                                wait_chunk(e, b, p, t, q)
                                e.tensor_copy(pT[:, t % 2, c0:c0 + w],
                                              rg[:, c0 // CH, 0:w]).then_inc(s_["pt_by_dve"], 1)
                            else:
                                e.memset(idle[:, :], 0.0).then_inc(s_["pt_by_dve"], 1)
                    if s > lag:
                        normalise(s - lag - 1)

        def load_parts(e, dst, col0, src, h, keys, done):
            at = 0
            for first, reps, n in (((0, 3, 1), (1, 2, 1), (2, 1, 1)) if keys else ((0, 1, 3), (0, 1, 2), (0, 1, 1))):
                rows_ = reps * n * HD
                s2 = src[bass.ds(h, 1), first * HD:(first + n) * HD, :].rearrange("a r s -> (a r) s")
                if keys:
                    for r in range(reps):
                        e.dma_start(dst[at:at + HD, col0:col0 + S], s2).then_inc(done, 16)
                        at += HD
                else:
                    e.dma_start(dst[at:at + rows_, col0:col0 + S], s2).then_inc(done, 16)
                    at += rows_

        def sp_attention(e, b, kind):
            s_ = AA if kind == "A" else BB

            def load_qk(h, hd):
                load_parts(e, qu_s[hd], 0, qu_d, h, False, s_[f"qk_loaded{hd}"])
                load_parts(e, k_s[hd], 0, k_d, h, True, s_[f"qk_loaded{hd}"])

            def load_qv(h, hd):
                load_parts(e, qv_s[hd], 0, qv_d, h, False, qv_loaded[hd])
                load_parts(e, pos_s[hd], 1, pos_d, h, True, qv_loaded[hd])

            def load_v(h, hd):
                e.dma_start(v_s[hd].rearrange("p t w -> p (t w)"),
                            v_d[bass.ds(h, 1)].rearrange("a p w -> (a p) w")).then_inc(s_[f"v_loaded{hd}"], 16)

            def strip_write(t, rb, db):
                k = t % RING
                for v in (e.snap(rb + (t + 1)),):
                    d = e.snap(db + 16 * (t // RING)) if t >= RING else None
                    e.wait_ge(r_free[4], v)
                    e.wait_ge(r_free[3], v)
                    if d is not None:
                        e.wait_ge(strip_in[k], d)
                    settle(e)
                e.dma_start(strip_d[k], strips[:, k * STRIP:(k + 1) * STRIP]).then_inc(strip_out[k], 16)

            def strip_read(t, T, db):
                k = t % RING
                d = e.snap(db + 16 * (t // RING + 1))
                v = e.snap(T + (t - RING + 1)) if t - 2 >= 2 else None
                e.wait_ge(strip_out[k], d)
                settle(e)
                if v is not None:
                    e.wait_ge(s_["pt_full3"], v)
                settle(e)
                skewed = bass.AP(tensor=strip_d.tensor, offset=k * P * STRIP + P - 1, ap=[[STRIP - 1, P], [1, S]])
                e.dma_start(z[:, k, :], skewed).then_inc(strip_in[k], 16)

            def load_next(p, T, hd):
                if hd:
                    v = e.snap(T + hd * NT)
                    e.wait_ge(s_["pv_done"], v)
                    settle(e)
                h = e.snap(p * HB + (hd + 1))
                load_qk(h, (hd + 1) % NB)
                load_v(h, (hd + 1) % NB)

            load_qk(0, 0)
            load_v(0, 0)
            if kind == "A":
                load_qv(0, 0)
                load_qv(1, 1)
                rb = e.snap(b * (nh * NT + AHEAD))
                db = e.snap(b * (16 * (nh * 4 + 1)))
                for t in range(AHEAD):
                    strip_write(t, rb, db)
                for t in range(2):
                    strip_read(t, 0, db)
            with e.Fori(0, nh // HB) as p:
                T = e.snap(b * (nh * NT) + p * G)
                if kind == "A":
                    rb = e.snap(b * (nh * NT + AHEAD) + p * G)
                    db = e.snap(b * (16 * (nh * 4 + 1)) + p * (16 * G // RING))
                v = e.snap(T + 1)
                e.wait_ge(s_["lo_ready"], v)
                settle(e)
                for s in range(G if kind == "A" else 0):
                    if s % NT == NT - AHEAD:
                        r = e.snap(rb + (s + AHEAD))
                        e.wait_ge(r_full[4], r)
                        settle(e)
                        load_qv(e.snap(p * HB + (s // NT + 2)), s // NT % NB)
                    strip_write(s + AHEAD, rb, db)
                    strip_read(s + 2, T, db)
                    if s % NT == 4:
                        load_next(p, T, s // NT)
                if kind == "B":
                    for hd in range(HB):
                        load_next(p, T, hd)
            if kind == "A":
                db = e.snap(b * (16 * (nh * 4 + 1)) + 16 * (nh * 4 + 1))
                e.wait_ge(strip_out[2], db)
                e.wait_ge(strip_out[3], db)
                v = e.snap(b * (nh * NT) + nh * NT)
                e.wait_ge(s_["pv_done"], v)
                settle(e)
                for k in (2, 3):
                    skewed = bass.AP(tensor=strip_d.tensor, offset=k * P * STRIP + P - 1, ap=[[STRIP - 1, P], [1, S]])
                    e.dma_start(z[:, k, :], skewed).then_inc(strip_in[k], 16)
                for k in range(RING):
                    e.wait_ge(strip_in[k], db)
                v = e.snap(b * (QK_INC * (nh // NB + 1)) + QK_INC * (nh // NB + 1))
                for hd in range(NB):
                    e.wait_ge(qv_loaded[hd], v)
                    settle(e)
            for name, per in (("qk_loaded", QK_INC), ("v_loaded", 16)):
                for hd in range(NB):
                    v = e.snap(b * (per * loads_of(hd)) + per * loads_of(hd))
                    e.wait_ge(s_[f"{name}{hd}"], v)
                    settle(e)

        def oc(b, kind):
            return b * (2 * NT) + (NT if kind == "B" else 0)

        def pe_out(e, b, kind):
            w = wA if kind == "A" else wB
            base = e.snap(oc(b, kind))

            def tr(t):
                if t >= 2:
                    e.wait_ge(oo_T, base + (t - 1))
                for m in range(KT):
                    mm = e.transpose(rg[:, t % 2, m * P:(m + 1) * P], attn[:, t, m * P:(m + 1) * P], ident[:, :])
                mm.then_inc(oo_tr, 1)

            tr(0)
            for t in range(NT):
                if t + 1 < NT:
                    tr(t + 1)
                e.wait_ge(oo_T, base + (t + 1))
                if t >= 4:
                    e.wait_ge(oo_sum, base + (t - 3))
                for k in range(KT):
                    mm = e.matmul(sc[:, t % 4, 0:D], aoT[:, t % 2, k, :], w[:, 3, k, :], start=k == 0,
                                  stop=k == KT - 1)
                mm.then_inc(oo_ready, 1)

        def act_out(e, b, kind):
            base = e.snap(oc(b, kind))
            for t in range(NT):
                e.wait_ge(oo_tr, base + (t + 1))
                if t >= 2:
                    e.wait_ge(oo_ready, base + (t - 1))
                e.activation(aoT[:, t % 2, :, :], rg[:, t % 2, 0:D].rearrange("p (k c) -> p k c", k=KT),
                             ACT.Copy).then_inc(oo_T, 1)

        def dve_out(e, b, kind):
            base = e.snap(oc(b, kind))
            for t in range(NT):
                e.wait_ge(oo_ready, base + (t + 1))
                e.tensor_tensor(x_res[:, t, :], sc[:, t % 4, 0:D], x_res[:, t, :], ALU.add).then_inc(oo_sum, 1)

        def pool_out(e, b, kind):
            base = e.snap(oc(b, kind))
            for t in range(NT):
                e.wait_ge(oo_sum, base + (t + 1))
                e.tensor_tensor(x_res[:, t, :], x_res[:, t, :], rows[:, ROWS["bo" if kind == "A" else "Bbo"], :],
                                ALU.add).then_inc(oo_added, 1)

        def fc(b, k, per):
            return b * (2 * per) + k * per

        def pe_ffn(e, b, k2):
            hb = e.snap(fc(b, k2, NC * NI))
            tb = e.snap(fc(b, k2, NT))

            def up(c):
                for i in range(NI):
                    n = c * NI + i
                    if n >= 4:
                        e.wait_ge(ff_relu, hb + (n - 3))
                    for k in range(KT):
                        mm = e.matmul(sc[:, n % 4, :], w1[:, k, i * P:(i + 1) * P], xnT[:, k, c * CH:(c + 1) * CH],
                                      start=k == 0, stop=k == KT - 1)
                    mm.then_inc(ff_h, 1)

            def down(c):
                e.wait_ge(ff_relu, hb + (c + 1) * NI)
                for t in range(4 * c, 4 * c + 4):
                    if t >= 3:
                        e.wait_ge(ff_sum, tb + (t - 2))
                    for i in range(NI):
                        mm = e.matmul(rg[:, t % 3, 0:D], hT[c % 2][:, i, (t - 4 * c) * P:(t - 4 * c + 1) * P],
                                      w2[:, i, :], start=i == 0, stop=i == NI - 1)
                    mm.then_inc(ff_ready, 1)

            up(0)
            for c in range(NC):
                if c + 1 < NC:
                    up(c + 1)
                down(c)

        def act_ffn(e, b, k2):
            hb = e.snap(fc(b, k2, NC * NI))
            tb = e.snap(fc(b, k2, NT))
            for c in range(NC):
                if c >= 2:
                    e.wait_ge(ff_ready, tb + 4 * (c - 1))
                for i in range(NI):
                    n = c * NI + i
                    e.wait_ge(ff_h, hb + (n + 1))
                    e.activation(hT[c % 2][:, i, :], sc[:, n % 4, :], ACT.Relu,
                                 bias=cols[:, COLS["b1"] + i:COLS["b1"] + i + 1]).then_inc(ff_relu, 1)

        def dve_ffn(e, b, k2):
            tb = e.snap(fc(b, k2, NT))
            for t in range(NT):
                e.wait_ge(ff_ready, tb + (t + 1))
                e.tensor_tensor(x_res[:, t, :], rg[:, t % 3, 0:D], x_res[:, t, :], ALU.add).then_inc(ff_sum, 1)

        def pool_ffn(e, b, k2):
            tb = e.snap(fc(b, k2, NT))
            for t in range(NT):
                e.wait_ge(ff_sum, tb + (t + 1))
                e.tensor_tensor(x_res[:, t, :], x_res[:, t, :], rows[:, ROWS["b2"], :], ALU.add).then_inc(ff_added, 1)

        block = ctx.enter_context(nc.Block())

        @block.sync
        def _(e):
            def wload(dst, src):
                e.dma_start(dst, src).then_inc(loaded, 16)

            for i, n in enumerate(("q", "k", "v", "o")):
                wload(wA[:, i], a["A_W" + n].rearrange("(k p) n -> p k n", p=P))
                wload(wB[:, i], a["B_W" + n + "T"].rearrange("(k p) n -> p k n", p=P))
            wload(wp[:, :, :], a["A_Wp"].rearrange("(k p) n -> p k n", p=P))
            wload(w1[:, :, :], a["W1"].rearrange("(k p) n -> p k n", p=P))
            wload(w2[:, :, :], a["W2"].rearrange("(k p) n -> p k n", p=P))
            wload(cols[:, :], a["cols"])
            wload(rows[:, :, :].rearrange("p r n -> p (r n)"),
                  a["rows"].rearrange("r n -> (r n)").rearrange("(a m) -> a m", a=1).to_broadcast([P, 5 * D]))
            wload(ident[:, :], a["ident"])
            wload(sel[:, :], a["sel"])
            wload(mask[:, S - P:S], a["tri"])
            wload(embT, a["embT"].rearrange("(k p) s -> p k s", p=P))
            zd = sem_zero
            e.wait_ge(zeroed, 8)
            for h in range(H, H + NB):
                for d in (qu_d, qv_d, k_d, pos_d):
                    e.dma_start(d[h], k_sb[0:PARTS * HD, :]).then_inc(zd, 16)
                e.dma_start(v_d[h], mask[:, 0:NT * VW]).then_inc(zd, 16)
            e.wait_ge(loaded, 16 * LOADS)
            e.wait_ge(zd, 16 * 5 * NB)
            sp_project(e, None, "pos")
            meet(e, None, 0)
            with e.Fori(0, nb) as b0:
                b = b0
                b1 = e.snap(b0 * 1)
                e.dma_start(x_res[:, :, :], a["x"][bass.ds(b0, 1)].rearrange("a (t p) n -> p (a t) n", p=P)).then_inc(
                    x_loaded, 16)
                v = e.snap(b * 16 + 16)
                e.wait_ge(x_loaded, v)
                meet_b(e, b, 1)
                meet_b(e, b, 2)
                sp_project(e, b, "A")
                sp_values(e, b, "A")
                meet_b(e, b, 3)
                sp_attention(e, b, "A")
                meet_b(e, b, 4)
                meet_b(e, b, 5)
                meet_b(e, b, 6)
                meet_b(e, b, 7)
                meet_b(e, b, 8)
                sp_project(e, b, "B")
                sp_values(e, b, "B")
                meet_b(e, b, 9)
                sp_attention(e, b, "B")
                meet_b(e, b, 10)
                meet_b(e, b, 11)
                meet_b(e, b, 12)
                meet_b(e, b, 13)
                e.dma_start(out[bass.ds(b0, 1)].rearrange("a (t p) n -> p (a t) n", p=P), x_res[:, :, :]).then_inc(
                    stored, 16)
                v = e.snap(b * 16 + 16)
                e.wait_ge(stored, v)
                settle(e)

        @block.gpsimd
        def _(e):
            e.memset(k_sb[:, :], 0.0).then_inc(zeroed, 1)
            for hd in range(NB):
                e.memset(qv_s[hd][:, S:S + 1], 0.0).then_inc(zeroed, 1)
                e.memset(pos_s[hd][:, 0:1], 0.0).then_inc(zeroed, 1)
            e.memset(mask[:, 0:S - P], 0.0).then_inc(zeroed, 1)
            e.memset(mhi[:, :], 0.0).then_inc(zeroed, 1)
            e.memset(mlo[:, :], 0.0).then_inc(zeroed, 1)
            e.wait_ge(loaded, 16 * LOADS)
            pool_project(e, None, "pos")
            meet(e, None, 0)
            with e.Fori(0, nb) as b:
                meet_b(e, b, 1)
                meet_b(e, b, 2)
                pool_project(e, b, "A")
                pool_values(e, b, "A")
                meet_b(e, b, 3)
                meet_b(e, b, 4)
                pool_out(e, b, "A")
                meet_b(e, b, 5)
                meet_b(e, b, 6)
                pool_ffn(e, b, 0)
                meet_b(e, b, 7)
                meet_b(e, b, 8)
                pool_project(e, b, "B")
                pool_values(e, b, "B")
                meet_b(e, b, 9)
                pool_attention(e, b, "B")
                meet_b(e, b, 10)
                pool_out(e, b, "B")
                meet_b(e, b, 11)
                meet_b(e, b, 12)
                pool_ffn(e, b, 1)
                meet_b(e, b, 13)

        @block.tensor
        def _(e):
            e.wait_ge(loaded, 16 * LOADS)
            pe_project(e, None, "pos", embT)
            meet(e, None, 0)
            with e.Fori(0, nb) as b:
                meet_b(e, b, 1)
                pe_norm(e, b, 0)
                meet_b(e, b, 2)
                pe_project(e, b, "A", xnT)
                pe_values(e, b, "A")
                meet_b(e, b, 3)
                pe_attention(e, b, "A")
                meet_b(e, b, 4)
                pe_out(e, b, "A")
                meet_b(e, b, 5)
                pe_norm(e, b, 1)
                meet_b(e, b, 6)
                pe_ffn(e, b, 0)
                meet_b(e, b, 7)
                pe_norm(e, b, 2)
                meet_b(e, b, 8)
                pe_project(e, b, "B", xnT)
                pe_values(e, b, "B")
                meet_b(e, b, 9)
                pe_attention(e, b, "B")
                meet_b(e, b, 10)
                pe_out(e, b, "B")
                meet_b(e, b, 11)
                pe_norm(e, b, 3)
                meet_b(e, b, 12)
                pe_ffn(e, b, 1)
                meet_b(e, b, 13)

        @block.scalar
        def _(e):
            e.wait_ge(loaded, 16 * LOADS)
            act_project(e, None, "pos")
            meet(e, None, 0)
            with e.Fori(0, nb) as b:
                meet_b(e, b, 1)
                act_norm(e, b, 0)
                meet_b(e, b, 2)
                act_project(e, b, "A")
                meet_b(e, b, 3)
                act_attention(e, b, "A")
                meet_b(e, b, 4)
                act_out(e, b, "A")
                meet_b(e, b, 5)
                act_norm(e, b, 1)
                meet_b(e, b, 6)
                act_ffn(e, b, 0)
                meet_b(e, b, 7)
                act_norm(e, b, 2)
                meet_b(e, b, 8)
                act_project(e, b, "B")
                meet_b(e, b, 9)
                act_attention(e, b, "B")
                meet_b(e, b, 10)
                act_out(e, b, "B")
                meet_b(e, b, 11)
                act_norm(e, b, 3)
                meet_b(e, b, 12)
                act_ffn(e, b, 1)
                meet_b(e, b, 13)

        @block.vector
        def _(e):
            e.wait_ge(loaded, 16 * LOADS)
            for dst, n in ((bqu, "u"), (bqv, "v")):
                e.tensor_tensor(dst[:, :], cols[:, COLS["bq"]:COLS["bq"] + KT], cols[:, COLS[n]:COLS[n] + KT],
                                ALU.add).then_inc(bias_ready, 1)
            dve_project(e, None, "pos")
            meet(e, None, 0)
            with e.Fori(0, nb) as b:
                meet_b(e, b, 1)
                dve_norm(e, b, 0)
                meet_b(e, b, 2)
                dve_project(e, b, "A")
                dve_values(e, b, "A")
                meet_b(e, b, 3)
                dve_attention(e, b, "A")
                meet_b(e, b, 4)
                dve_out(e, b, "A")
                meet_b(e, b, 5)
                dve_norm(e, b, 1)
                meet_b(e, b, 6)
                dve_ffn(e, b, 0)
                meet_b(e, b, 7)
                dve_norm(e, b, 2)
                meet_b(e, b, 8)
                dve_project(e, b, "B")
                dve_values(e, b, "B")
                meet_b(e, b, 9)
                dve_attention(e, b, "B")
                meet_b(e, b, 10)
                dve_out(e, b, "B")
                meet_b(e, b, 11)
                dve_norm(e, b, 3)
                meet_b(e, b, 12)
                dve_ffn(e, b, 1)
                meet_b(e, b, 13)


def constants():
    pos = np.arange(S, dtype=np.float32)
    idx = np.arange(D // 2, dtype=np.float32)
    inv_freq = np.float32(1.0) / np.float32(10000.0) ** (np.float32(2.0) * idx / np.float32(D))
    ang = pos[:, None] * inv_freq[None, :].astype(np.float32)
    emb = np.concatenate([np.sin(ang), np.cos(ang)], axis=-1).astype(np.float32)
    sel = np.zeros((P, VW), np.float32)
    for p in range(P):
        sel[p, p % VW] = 1.0
    tri = np.where(np.arange(P)[None, :] > np.arange(P)[:, None], NEG, 0.0).astype(np.float32)
    return {"embT": np.ascontiguousarray(emb.T), "ident": np.eye(P, dtype=np.float32), "sel": sel, "tri": tri}


def arrays_of(i):
    c = np.ascontiguousarray

    def two(x):
        return np.asarray(x).reshape(-1, P).T

    arr = {"x": c(i["L0_attn_a_x"])}
    for n in "qkvpo":
        arr["A_W" + n] = c(i["L0_attn_a_W" + n])
    for n in "qkvo":
        arr["B_W" + n + "T"] = c(np.asarray(i["L0_attn_b_W" + n]).T)
    arr["W1"] = c(i["L0_ffn_W1"])
    arr["W2"] = c(i["L0_ffn_W2"])
    arr["cols"] = c(np.concatenate([two(i[n]) for n in (
        "L0_attn_a_bq", "L0_attn_a_bk", "L0_attn_a_bp", "L0_attn_a_u", "L0_attn_a_v", "L0_attn_b_bq",
        "L0_attn_b_bk", "L0_ffn_b1")], axis=1))
    arr["rows"] = c(np.stack([np.asarray(i[n]) for n in (
        "L0_attn_a_bv", "L0_attn_a_bo", "L0_attn_b_bv", "L0_attn_b_bo", "L0_ffn_b2")]))
    arr.update(constants())
    return arr


def kernel(**inputs):
    import concourse.bacc as bacc
    from concourse.bass_utils import run_bass_kernel_spmd

    nc = bacc.Bacc("TRN2", target_bir_lowering=False, num_devices=1)
    arrays = {"in_" + n: v for n, v in arrays_of(inputs).items()}
    aps = {n[3:]: nc.dram_tensor(n, v.shape, mybir.dt.from_np(v.dtype), kind="ExternalInput").ap()
           for n, v in arrays.items()}
    shape = inputs["L0_attn_a_x"].shape
    out = nc.dram_tensor("out_0_dram", shape, F32, kind="ExternalOutput").ap()
    program(nc, aps, out)
    r = run_bass_kernel_spmd(nc, [arrays], core_ids=[0])
    return r.results[0]["out_0_dram"]
```

```python
from contextlib import ExitStack

import numpy as np

import concourse.bass as bass
from concourse import mybir

F32 = mybir.dt.float32
BF16 = mybir.dt.bfloat16
ALU = mybir.AluOpType
ACT = mybir.ActivationFunctionType
AX = mybir.AxisListType

P = 128
D = 256
KT = D // P
H = 16
HD = D // H
S = 2048
NT = S // P
CH = 512
NC = S // CH
XN = 3
QT = NT // NC
INTER = 1024
NI = INTER // P
PARTS = 3
SLOTS = 6
KROWS = SLOTS * HD
STRIP = S + P
RING = 4
AHEAD = 4
VW = 32
SCALE = 1.0 / float(np.sqrt(HD))
EPS = 1e-5
NEG = -1.0e30

R_CHUNKS = [(c * CH, min(CH, STRIP - c * CH)) for c in range(5)]
R_BANK = [0, 1, 2, 0, 1]
R_BY_DVE = [3]
P_BANK = [2, 0, 1, 2]
P_BY_DVE = [0, 1]
HB = 4
NB = 2
G = HB * NT
LAG = dict(A=1, B=2)
OB = 4
EARLY = NT // 2 - 1
B_BANK = [0, 1, 2, 0]

COLS = dict(bq=0, bk=2, bp=4, u=6, v=8, Bbq=10, Bbk=12, b1=14)
NCOLS = 22
ROWS = dict(bv=0, bo=1, Bbv=2, Bbo=3, b2=4)


def program(nc, a, out, nb=4, nh=H):
    ctx = ExitStack()
    with ctx:
        def sb(name, shape, dt=F32):
            return ctx.enter_context(nc.sbuf_tensor(name, shape, dt))

        def pb(name, shape):
            return ctx.enter_context(nc.psum_tensor(name, shape, F32))

        def sem(name):
            return ctx.enter_context(nc.semaphore(name))

        qu_d = nc.dram_tensor("qu_parts", (H + NB, PARTS * HD, S), BF16).ap()
        qv_d = nc.dram_tensor("qv_parts", (H + NB, PARTS * HD, S), BF16).ap()
        k_d = nc.dram_tensor("k_parts", (H + NB, PARTS * HD, S), BF16).ap()
        pos_d = nc.dram_tensor("pos_parts", (H + NB, PARTS * HD, S), BF16).ap()
        v_d = nc.dram_tensor("v_heads", (H + NB, P, NT * VW), F32).ap()
        strip_d = nc.dram_tensor("strips", (RING, P, STRIP), F32).ap()

        x_res = sb("x_res", [P, NT, D])
        xnT = sb("xnT", [P, KT, S])
        attn = sb("attn", [P, NT, D])
        qv_s = [sb("qv_s0", [KROWS, S + 1], BF16), sb("qv_s1", [KROWS, S + 1], BF16)]
        pos_s = [sb("pos_s0", [KROWS, S + 1], BF16), sb("pos_s1", [KROWS, S + 1], BF16)]
        k_sb = sb("k_sb", [KROWS, S], BF16)
        strips = sb("strips_sb", [P, RING * STRIP])
        z = sb("z", [P, RING, S])
        pT = sb("pT", [P, 2, S])
        po_sb = sb("po_sb", [P, OB, P])
        rsum = sb("rsum", [P, OB])
        mlo = sb("mlo", [P, 2])
        mhi = sb("mhi", [P, 2])
        nmax = sb("nmax", [P, 2])
        idle = sb("idle", [P, 1])
        wA = sb("wA", [P, 4, KT, D])
        wB = sb("wB", [P, 4, KT, D])
        wp = sb("wp", [P, KT, D])
        w1 = sb("w1", [P, KT, INTER])
        w2 = sb("w2", [P, NI, D])
        cols = sb("cols", [P, NCOLS])
        rows = sb("rows", [P, 5, D])
        ident = sb("ident", [P, P])
        sel = sb("sel", [P, VW])
        mask = sb("mask", [P, S])
        bqu = sb("bqu", [P, KT])
        bqv = sb("bqv", [P, KT])
        stats = sb("stats", [P, NT, 6])
        mv = sb("mv", [P, NT, 2])
        ve = sb("ve", [P, NT])
        rstd = sb("rstd", [P, NT])
        nwt = sb("nwt", [P, 3, NT])
        xn = sb("xn", [P, XN, D])
        aoT = sb("aoT", [P, 2, KT, P])

        xnT_f = xnT[:, :, :].rearrange("p k s -> p (k s)")
        qk2 = xnT_f[0:KROWS, 0:S].bitcast(BF16)
        v_at = [S + i * NT * VW for i in range(NB)]
        qu_at = S + NB * NT * VW
        qu_s = [xnT_f[0:KROWS, qu_at:qu_at + S // 2].bitcast(BF16), qk2[:, 0:S]]
        k_s = [k_sb[:, :], qk2[:, S:2 * S]]
        v_s = [xnT_f[:, at:at + NT * VW].rearrange("p (t w) -> p t w", t=NT) for at in v_at]

        zf = z[:, :, :].rearrange("p r s -> p (r s)")
        zb = zf.bitcast(BF16)
        pb16 = pT[:, :, :].rearrange("p r s -> p (r s)").bitcast(BF16)
        parts = ([[zb[:, (k * PARTS + i) * S:(k * PARTS + i + 1) * S] for i in range(PARTS)] for k in range(2)]
                 + [[pb16[:, i * S:(i + 1) * S] for i in range(PARTS)]])
        SETS = len(parts)
        resid = [zf[:, 3 * S + i * CH:3 * S + (i + 1) * CH] for i in range(4)]
        v_all = strips[:, 0:H * NT * VW].rearrange("p (h t w) -> p h t w", h=H, t=NT)
        hT = [strips[:, i * NI * CH:(i + 1) * NI * CH].rearrange("p (n c) -> p n c", n=NI) for i in range(2)]
        embT = strips[:, 0:KT * S].rearrange("p (k s) -> p k s", k=KT)

        sc = pb("sc", [P, 4, CH])
        rg = pb("rg", [P, 3, CH])
        op = pb("op", [P, CH])
        po = op[:, 0:P]
        on = op[:, P:P + OB * VW].rearrange("p (o w) -> p o w", o=OB)
        scf = sc[:, :, :].rearrange("p b c -> p (b c)")

        phase_done = sem("phase_done")
        waited = sem("waited")
        loaded = sem("loaded")
        zeroed = sem("zeroed")
        bias_ready = sem("bias_ready")
        x_loaded = [sem(f"x_loaded{c}") for c in range(NC)]
        stored = [sem(f"stored{c}") for c in range(NC)]
        ln_stat = sem("ln_stat")
        ln_var = sem("ln_var")
        ln_sqrt = sem("ln_sqrt")
        ln_step = sem("ln_step")
        ln_xn = sem("ln_xn")
        ln_tr = sem("ln_tr")
        ln_out = sem("ln_out")
        pj_ready = sem("pj_ready")
        pj_high = sem("pj_high")
        pj_resid = sem("pj_resid")
        pj_mid = sem("pj_mid")
        pj_low = sem("pj_low")
        pj_stored = [sem(f"pj_stored{k}") for k in range(3)]
        pv_ready = sem("pv_ready")
        pv_added = sem("pv_added")
        pv_pad = sem("pv_pad")
        pv_stored = sem("pv_stored")
        oo_tr = sem("oo_tr")
        oo_T = sem("oo_T")
        oo_ready = sem("oo_ready")
        oo_sum = sem("oo_sum")
        oo_added = sem("oo_added")
        ff_h = sem("ff_h")
        ff_relu = sem("ff_relu")
        ff_ready = sem("ff_ready")
        ff_sum = sem("ff_sum")
        ff_added = sem("ff_added")
        names = ["lo_ready", "hi_ready", "lo_read", "hi_read", "maxes", "nmax_ready", "exp_done", "pv_done",
                 "po_copied", "comb_done", "rcp", "out_read", "qk_loaded0", "qk_loaded1", "v_loaded0", "v_loaded1"]
        AA = {n: sem("A_" + n) for n in names}
        BB = {n: sem("B_" + n) for n in names}
        for q in range(4):
            AA[f"pt_full{q}"] = sem(f"A_pt_full{q}")
            AA[f"pt_free{q}"] = sem(f"A_pt_free{q}")
        for n in ("pt_by_act", "pt_by_dve"):
            BB[n] = sem("B_" + n)
        r_full = [sem(f"r_full{c}") for c in range(5)]
        r_free = [sem(f"r_free{c}") for c in range(5)]
        strip_out = [sem(f"strip_out{k}") for k in range(RING)]
        strip_in = [sem(f"strip_in{k}") for k in range(RING)]
        qv_loaded = [sem("qv_loaded0"), sem("qv_loaded1")]
        sem_zero = sem("spare_head_zero")

        PHASES = 9
        ENG = 5
        LOADS = 17
        QK_INC = 16 * (3 + 6)

        def meet(e, b, k):
            e.drain().then_inc(phase_done, 1)
            e.wait_ge(phase_done, ENG)

        def settle(e):
            e.sem_inc(waited, 1)

        def meet_b(e, b, k):
            v = e.snap(b * (ENG * PHASES) + ENG * (k + 1))
            settle(e)
            e.drain().then_inc(phase_done, 1)
            e.wait_ge(phase_done, v)
            settle(e)

        def jobs(kind):
            if kind == "pos":
                return [(wp[:, :, :], cols[:, COLS["bp"] + m:COLS["bp"] + m + 1], pos_d, m) for m in range(KT)]
            if kind == "A":
                return ([(wA[:, 0], bias[:, m:m + 1], dst, m) for m in range(KT)
                         for bias, dst in ((bqu, qu_d), (bqv, qv_d))]
                        + [(wA[:, 1], cols[:, COLS["bk"] + m:COLS["bk"] + m + 1], k_d, m) for m in range(KT)])
            return ([(wB[:, 0], cols[:, COLS["Bbq"] + m:COLS["Bbq"] + m + 1], qu_d, m) for m in range(KT)]
                    + [(wB[:, 1], cols[:, COLS["Bbk"] + m:COLS["Bbk"] + m + 1], k_d, m) for m in range(KT)])

        NJ = {"pos": 2, "A": 6, "B": 4}
        JB = NJ["A"] + NJ["B"]
        JOFF = {"pos": 0, "A": NJ["pos"], "B": NJ["pos"] + NJ["A"]}

        def shared(kind, j):
            return kind == "A" and j in (1, 3)

        def products(b, kind, j):
            before = sum(not shared(kind, i) for i in range(j + 1)) - 1
            if kind == "pos":
                return before * NC
            return b * ((JB - 2) * NC) + (NJ["pos"] + (NJ["A"] - 2 if kind == "B" else 0) + before) * NC

        def jbase(b, kind):
            return JOFF[kind] if kind == "pos" else b * JB + JOFF[kind]

        NORM_OF = dict(A=0, B=2)

        def pe_project(e, b, kind, src):
            if kind != "pos":
                pe_norm_tiles(e, b, NORM_OF[kind], range(NT))
            jb = jbase(b, kind)
            for j, (w, _, _, m) in enumerate(jobs(kind)):
                if shared(kind, j):
                    continue
                for c in range(NC):
                    n = j * NC + c
                    if j == 0 and kind != "pos":
                        wait_norm(e, b, NORM_OF[kind], c)
                    if n >= 4:
                        e.wait_ge(pj_resid, jb * NC + (n - 3))
                    for k in range(KT):
                        mm = e.matmul(sc[:, c, :], w[:, k, m * P:(m + 1) * P], src[:, k, c * CH:(c + 1) * CH],
                                      start=k == 0, stop=k == KT - 1)
                    mm.then_inc(pj_ready, 1)

        def act_project(e, b, kind):
            jb = jbase(b, kind)

            def mid(n):
                j, c = n // NC, n % NC
                e.wait_ge(pj_resid, jb * NC + (n + 1))
                e.activation(parts[j % SETS][1][:, c * CH:(c + 1) * CH], resid[c], ACT.Copy).then_inc(pj_mid, 1)

            if kind != "pos":
                act_norm_tiles(e, b, NORM_OF[kind], range(NT))
            for j, (_, bias, _, m) in enumerate(jobs(kind)):
                for c in range(NC):
                    n = j * NC + c
                    if c == 0 and j >= SETS:
                        e.wait_ge(pj_stored[j % SETS], pj_count(b, kind, j - SETS))
                    e.wait_ge(pj_ready, products(b, kind, j) + (c + 1))
                    e.activation(parts[j % SETS][0][:, c * CH:(c + 1) * CH], sc[:, c, :], ACT.Identity,
                                 bias=bias).then_inc(pj_high, 1)
                    if n >= 1:
                        mid(n - 1)
            mid(NJ[kind] * NC - 1)

        def dve_project(e, b, kind):
            jb = jbase(b, kind)
            if kind != "pos":
                dve_norm_tiles(e, b, NORM_OF[kind])
            for j, (_, bias, _, m) in enumerate(jobs(kind)):
                for c in range(NC):
                    n = j * NC + c
                    e.wait_ge(pj_high, jb * NC + (n + 1))
                    if n >= 4:
                        e.wait_ge(pj_low, jb * NC + (n - 3))
                    e.scalar_tensor_tensor(out=resid[c], in0=sc[:, c, :], scalar=bias,
                                           in1=parts[j % SETS][0][:, c * CH:(c + 1) * CH],
                                           op0=ALU.add, op1=ALU.subtract).then_inc(pj_resid, 1)

        def pool_project(e, b, kind):
            jb = jbase(b, kind)
            for j in range(NJ[kind]):
                if j >= SETS:
                    e.wait_ge(pj_stored[j % SETS], pj_count(b, kind, j - SETS))
                for c in range(NC):
                    n = j * NC + c
                    cs = slice(c * CH, (c + 1) * CH)
                    e.wait_ge(pj_mid, jb * NC + (n + 1))
                    e.tensor_tensor(parts[j % SETS][2][:, cs], resid[c], parts[j % SETS][1][:, cs],
                                    ALU.subtract).then_inc(pj_low, 1)

        def pj_count(b, kind, j):
            def in_set(k):
                return len(range(j % SETS, NJ[k], SETS))

            per = 16 * PARTS
            js = per * (j // SETS + 1)
            if kind == "pos":
                return js
            return b * (per * (in_set("A") + in_set("B"))) + per * (in_set("pos") + (in_set("A") if kind == "B" else 0)) + js

        def sp_project(e, b, kind):
            jb = jbase(b, kind)
            for j, (_, _, dst, m) in enumerate(jobs(kind)):
                e.wait_ge(pj_low, jb * NC + (j + 1) * NC)
                settle(e)
                hs = dst[m * (H // KT):(m + 1) * (H // KT), :, :].rearrange("h (a d) s -> a h d s", a=PARTS)
                for i in range(PARTS):
                    e.dma_start(hs[i], parts[j % SETS][i]).then_inc(pj_stored[j % SETS], 16)
            for j in range(max(0, NJ[kind] - SETS), NJ[kind]):
                e.wait_ge(pj_stored[j % SETS], pj_count(b, kind, j))
                settle(e)

        def vcount(b, kind, per):
            return b * (2 * per) + (per if kind == "B" else 0)

        def pe_values(e, b, kind):
            w = wA if kind == "A" else wB
            base = vcount(b, kind, NT)
            for t in range(NT):
                if t >= 3:
                    e.wait_ge(pv_added, base + (t - 2))
                for k in range(KT):
                    mm = e.matmul(rg[:, t % 3, 0:D], xnT[:, k, t * P:(t + 1) * P], w[:, 2, k, :],
                                  start=k == 0, stop=k == KT - 1)
                mm.then_inc(pv_ready, 1)

        def dve_values(e, b, kind):
            bv = rows[:, ROWS["bv" if kind == "A" else "Bbv"], :].rearrange("p (h d) -> p h d", h=H)
            base = vcount(b, kind, NT)
            for t in range(NT):
                e.wait_ge(pv_ready, base + (t + 1))
                e.tensor_tensor(v_all[:, :, t, 0:HD], rg[:, t % 3, 0:D].rearrange("p (h d) -> p h d", h=H), bv,
                                ALU.add).then_inc(pv_added, 1)

        def pool_values(e, b, kind):
            e.memset(v_all[:, :, :, HD + 1:VW], 0.0).then_inc(pv_pad, 1)
            e.memset(v_all[:, :, :, HD:HD + 1], 1.0).then_inc(pv_pad, 1)

        def sp_values(e, b, kind):
            e.wait_ge(pv_added, vcount(b, kind, NT) + NT)
            settle(e)
            e.wait_ge(pv_pad, vcount(b, kind, 2) + 2)
            e.dma_start(v_d[0:H].rearrange("h p w -> p h w"),
                        strips[:, 0:H * NT * VW].rearrange("p (h w) -> p h w", h=H)).then_inc(pv_stored, 16)
            e.wait_ge(pv_stored, vcount(b, kind, 16) + 16)

        def lc(b, k, per):
            return b * (4 * per) + k * per

        def row_stats(e, t):
            e.bn_stats(stats[:, t, :], x_res[:, t, :]).then_inc(ln_stat, 1)

        def row_moments(e, b, k, t):
            e.wait_ge(ln_stat, lc(b, k, NT) + (t + 1))
            settle(e)
            e.bn_aggr(mv[:, t, :], stats[:, t, :]).then_inc(ln_var, 1)

        def stats_behind(e, b, k, t, added, base):
            if 1 <= t <= NT:
                e.wait_ge(added, base + t)
                settle(e)
                row_stats(e, t - 1)
            if t >= 2:
                row_moments(e, b, k, t - 2)

        def dve_norm(e, b, k):
            if k == 0:
                for t in range(NT + 1):
                    if t < NT:
                        row_stats(e, t)
                    if t >= 1:
                        row_moments(e, b, k, t - 1)
            e.wait_ge(ln_var, lc(b, k, NT) + NT)
            base = lc(b, k, 6)
            e.tensor_scalar(ve[:, :], mv[:, :, 1], EPS, None, ALU.add).then_inc(ln_step, 1)
            e.wait_ge(ln_sqrt, lc(b, k, 1) + 1)
            e.reciprocal(nwt[:, 1, :], nwt[:, 0, :]).then_inc(ln_step, 1)
            e.wait_ge(ln_step, base + 2)
            e.tensor_tensor(nwt[:, 2, :], nwt[:, 1, :], nwt[:, 1, :], ALU.mult).then_inc(ln_step, 1)
            e.wait_ge(ln_step, base + 3)
            e.tensor_tensor(nwt[:, 2, :], nwt[:, 2, :], ve[:, :], ALU.mult).then_inc(ln_step, 1)
            e.wait_ge(ln_step, base + 4)
            e.tensor_scalar(nwt[:, 2, :], nwt[:, 2, :], -0.5, 1.5, ALU.mult, ALU.add).then_inc(ln_step, 1)
            e.wait_ge(ln_step, base + 5)
            e.tensor_tensor(rstd[:, :], nwt[:, 2, :], nwt[:, 1, :], ALU.mult).then_inc(ln_step, 1)
            e.wait_ge(ln_step, base + 6)

        def dve_norm_tiles(e, b, k):
            for t in range(NT):
                if t >= XN:
                    e.wait_ge(ln_tr, lc(b, k, NT) + (t - XN + 1))
                e.tensor_scalar(xn[:, t % XN, :], x_res[:, t, :], mv[:, t, 0:1], rstd[:, t:t + 1],
                                ALU.subtract, ALU.mult).then_inc(ln_xn, 1)

        def act_norm(e, b, k):
            e.wait_ge(ln_step, lc(b, k, 6) + 1)
            e.activation(nwt[:, 0, :], ve[:, :], ACT.Sqrt).then_inc(ln_sqrt, 1)

        def act_norm_tiles(e, b, k, tiles):
            for t in tiles:
                e.wait_ge(ln_tr, lc(b, k, NT) + (t + 1))
                e.activation(xnT[:, :, t * P:(t + 1) * P], rg[:, t % 3, 0:D].rearrange("p (k c) -> p k c", k=KT),
                             ACT.Copy).then_inc(ln_out, 1)

        def pe_norm_tiles(e, b, k, tiles):
            for t in tiles:
                e.wait_ge(ln_xn, lc(b, k, NT) + (t + 1))
                if t >= 3:
                    e.wait_ge(ln_out, lc(b, k, NT) + (t - 2))
                for m in range(KT):
                    mm = e.transpose(rg[:, t % 3, m * P:(m + 1) * P], xn[:, t % XN, m * P:(m + 1) * P], ident[:, :])
                mm.then_inc(ln_tr, 1)

        def wait_norm(e, b, k, c):
            e.wait_ge(ln_out, lc(b, k, NT) + (c + 1) * QT)

        def loads_of(k):
            return nh // NB + (1 if k == 0 else 0)

        def load_count(b, p, hd, inc):
            return b * (inc * loads_of(hd % NB)) + p * (HB // NB * inc) + (hd // NB + 1) * inc

        def pe_attention(e, b, kind):
            s_ = AA if kind == "A" else BB
            lag = LAG[kind]

            def strip(t, rb, qv_at, chunks=range(5)):
                hd = t // NT % NB
                i0 = (t % NT) * P
                edge = i0 + P
                if t % NT == 0 and 0 in chunks:
                    e.wait_ge(qv_loaded[hd], qv_at + QK_INC * (t // NT // NB))
                for c in chunks:
                    c0, w = R_CHUNKS[c]
                    bank = R_BANK[c]
                    claim(bank)
                    for lo, hi, first in ((c0, min(c0 + w, edge), True), (max(c0, edge), c0 + w, False)):
                        if lo >= hi:
                            continue
                        if first:
                            q = qv_s[hd][:, i0:i0 + P]
                            m0 = 1 + S - P - i0 + lo
                        else:
                            q = qv_s[hd][:, i0 + 1:i0 + P + 1]
                            m0 = lo - edge
                        mm = e.matmul(rg[:, bank, lo - c0:hi - c0], q, pos_s[hd][:, m0:m0 + hi - lo],
                                      start=True, stop=True)
                    mm.then_inc(r_full[c], 1)
                    last[bank] = (r_free[c], rb + (t + 1))

            last = {}

            def claim(bank):
                if bank in last:
                    e.wait_ge(*last.pop(bank))

            if kind == "A":
                rb = e.snap(b * (nh * NT + AHEAD))
                for t in range(AHEAD):
                    strip(t, rb, b * (QK_INC * (nh // NB + 1)) + QK_INC)
                for bank in range(3):
                    claim(bank)
                settle(e)

            def content(g):
                s, hd = g % NT, g // NT
                if s == 0:
                    e.wait_ge(s_[f"qk_loaded{hd % NB}"], load_count(b, p, hd, QK_INC))
                width = S if kind == "A" else (s + 1) * P
                for half, ready, read in halves_of(kind, g):
                    c0s = [c for c in (0, 1) if c * CH < width - (2 * half * CH if width > 2 * CH else 0)]
                    if kind == "B" and NT // 2 <= s < NT // 2 + 1 and half == 1:
                        e.wait_ge(s_["lo_read"], T + g)
                    elif kind == "B" and 2 <= s <= NT // 2:
                        e.wait_ge(s_["lo_read"], T + (g - 1))
                    elif g >= 1:
                        n = halves_before(kind, g, half)
                        if n:
                            e.wait_ge(s_[read if s >= 2 or kind == "A" else ("lo_read", "hi_read")[half]],
                                      hbase(kind, T, b, p, half) + n)
                    for c in c0s:
                        k0 = c * CH + (2 * half * CH if width > 2 * CH else 0)
                        w = min(CH, width - k0)
                        mm = e.matmul(sc[:, 2 * half + c, 0:w], qu_s[hd % NB][:, s * P:(s + 1) * P],
                                      k_s[hd % NB][:, k0:k0 + w], start=True, stop=True)
                    mm.then_inc(s_[ready], 1)

            def combine(t):
                ng = 4 if kind == "A" else min(4, t % NT + 1)
                e.wait_ge(s_["po_copied"], T + (t + 1))
                mm = e.matmul(on[:, t % OB, :], po_sb[0:32 * ng, t % OB, :], sel[0:32 * ng, :], start=True, stop=True)
                if t % OB == OB - 1:
                    mm.then_inc(s_["comb_done"], 1)

            with e.Fori(0, nh // HB) as p:
                T = e.snap(b * (nh * NT) + p * G)
                U = e.snap(b * (nh * NT // OB) + p * (G // OB))
                last.clear()
                if kind == "A":
                    rb = e.snap(b * (nh * NT + AHEAD) + p * G)
                    ql = e.snap(b * (QK_INC * (nh // NB + 1)) + p * (HB // NB * QK_INC) + QK_INC)
                content(0)
                for s in range(G + lag + 1):
                    if kind == "A" and s < G:
                        strip(s + AHEAD, rb, ql, (0, 1))
                    early = kind == "B" and s + 1 < G and 2 <= (s + 1) % NT <= EARLY
                    if early:
                        content(s + 1)
                    if s > lag and (s - lag - 1) % NT == 0:
                        hd = (s - lag - 1) // NT
                        e.wait_ge(s_[f"v_loaded{hd % NB}"], load_count(b, p, hd, 16))
                    if s > lag:
                        t = s - lag - 1
                        if t % OB:
                            combine(t - 1)
                        elif t >= OB:
                            e.wait_ge(s_["out_read"], U + t // OB)
                        if kind == "A":
                            e.wait_ge(s_["pt_free1"], T + (t + 1))
                            e.wait_ge(s_["pt_free3"], T + (t + 1))
                        else:
                            e.wait_ge(s_["pt_by_act"], T + (t + 1))
                            e.wait_ge(s_["pt_by_dve"], T + (t + 1))
                        nj = NT if kind == "A" else t % NT + 1
                        nj4 = max(nj, 4) if kind == "A" else nj
                        for j in range(nj4):
                            g = j % 4
                            mm = e.matmul(po[32 * g:32 * g + 32, :], v_s[t // NT % NB][:, j, :], pT[:, t % 2, j * P:(j + 1) * P],
                                          start=j < 4, stop=j + 4 >= nj)
                        mm.then_inc(s_["pv_done"], 1)
                    if kind == "A":
                        if s < G:
                            strip(s + AHEAD, rb, ql, (2,))
                        if s + 1 < G:
                            content(s + 1)
                        if s > lag and (s - lag) % OB == 0:
                            combine(s - lag - 1)
                        if s < G:
                            strip(s + AHEAD, rb, ql, (3, 4))
                    if lag <= s < G + lag:
                        t = s - lag
                        e.wait_ge(s_["exp_done"], T + (t + 1))
                        nblk = NT if kind == "A" else t % NT + 1
                        if kind == "B" and t >= 1:
                            e.wait_ge(s_["pt_by_act"], T + t)
                            e.wait_ge(s_["pt_by_dve"], T + t)
                        for q in range(4):
                            blks = range(4 * q, min(4 * q + 4, nblk))
                            if not len(blks):
                                continue
                            if kind == "A":
                                bank = P_BANK[q]
                                claim(bank)
                            else:
                                bank = B_BANK[q]
                                if q == 3:
                                    e.wait_ge(pt_first, b * (nh * 4) + p * (HB * 4) + four_chunk(t))
                            for j in blks:
                                mm = e.transpose(rg[:, bank, (j - 4 * q) * P:(j - 4 * q + 1) * P],
                                                 z[:, t % RING, j * P:(j + 1) * P], ident[:, :])
                            if kind == "A":
                                mm.then_inc(s_[f"pt_full{q}"], 1)
                                last[bank] = (s_[f"pt_free{q}"], T + (t + 1))
                            else:
                                mm.then_inc(b_full[q], 1)
                    if kind == "B":
                        if s > lag and (s - lag) % OB == 0:
                            combine(s - lag - 1)
                        if s + 1 < G and not early:
                            content(s + 1)

        pt_first = sem("B_pt_first")
        b_full = [sem(f"B_pt_full{q}") for q in range(4)]

        def chunk_base(b, p, q):
            return b * (nh * (NT - 4 * q)) + p * (HB * (NT - 4 * q))

        def chunk_count(t, q):
            return t // NT * (NT - 4 * q) + t % NT - 4 * q + 1

        def wait_chunk(e, b, p, t, q):
            e.wait_ge(b_full[q], chunk_base(b, p, q) + chunk_count(t, q))

        def halves_of(kind, g):
            if kind == "B" and g % NT < NT // 2:
                return [(g % NT % 2, "lo_ready", "lo_read")]
            return [(0, "lo_ready", "lo_read"), (1, "hi_ready", "hi_read")]

        def halves_before(kind, g, half):
            if kind == "A" or half == 0:
                return g
            return g // NT * (NT // 2) + max(0, g % NT - NT // 2)

        def hbase(kind, T, b, p, half):
            if kind == "A" or half == 0:
                return T
            return b * (nh * (NT // 2)) + p * (HB * (NT // 2))

        def four_chunk(t):
            return t // NT * 4 + t % NT - 11

        def move_strip(e, op_copy, c, t, rb, wb):
            c0, w = R_CHUNKS[c]
            e.wait_ge(r_full[c], rb + (t + 1))
            if t >= RING and (c == 3 or c == 0):
                e.wait_ge(strip_out[t % RING], wb + 16 * (t // RING))
            k = t % RING
            op_copy(strips[:, k * STRIP + c0:k * STRIP + c0 + w], rg[:, R_BANK[c], 0:w]).then_inc(r_free[c], 1)

        def act_copy(e):
            return lambda o, i: e.activation(o, i, ACT.Copy)

        def act_attention(e, b, kind):
            s_ = AA if kind == "A" else BB
            lag = LAG[kind]
            if kind == "A":
                rb = e.snap(b * (nh * NT + AHEAD))
                for t in range(AHEAD):
                    for c in range(5):
                        if c not in R_BY_DVE:
                            move_strip(e, act_copy(e), c, t, rb, 0)
            with e.Fori(0, nh // HB) as p:
                T = e.snap(b * (nh * NT) + p * G)
                if kind == "A":
                    rb = e.snap(b * (nh * NT + AHEAD) + p * G)
                    wb = e.snap(b * (16 * (nh * 4 + 1)) + p * (16 * G // RING))
                for s in range(G + lag):
                    if kind == "A" and s < G:
                        for c in range(5):
                            if c not in R_BY_DVE:
                                move_strip(e, act_copy(e), c, s + AHEAD, rb, wb)
                    if kind == "A" and s < G:
                        w = S
                        e.wait_ge(s_["nmax_ready"], T + (s + 1))
                        e.activation(z[:, s % RING, 0:w], z[:, s % RING, 0:w], ACT.Exp,
                                     bias=nmax[:, s % 2:s % 2 + 1], scale=SCALE).then_inc(s_["exp_done"], 1)
                    if lag <= s:
                        t = s - lag
                        if t >= 2:
                            e.wait_ge(s_["pv_done"], T + (t - 1))
                        if kind == "A":
                            for q in range(4):
                                if q in P_BY_DVE:
                                    continue
                                e.wait_ge(s_[f"pt_full{q}"], T + (t + 1))
                                e.activation(pT[:, t % 2, q * CH:(q + 1) * CH], rg[:, P_BANK[q], :],
                                             ACT.Copy).then_inc(s_[f"pt_free{q}"], 1)
                        else:
                            nblk = t % NT + 1
                            for q in (0, 1, 3):
                                if nblk <= 4 * q or (q == 1 and nblk <= 8):
                                    continue
                                wait_chunk(e, b, p, t, q)
                                w = min(CH, nblk * P - q * CH)
                                mm = e.activation(pT[:, t % 2, q * CH:q * CH + w], rg[:, B_BANK[q], 0:w], ACT.Copy)
                                if q == 0 and nblk > 12:
                                    mm.then_inc(pt_first, 1)
                                    mm = None
                            mm.then_inc(s_["pt_by_act"], 1)
                    if kind == "B" and s < G:
                        w = (s % NT + 1) * P
                        e.wait_ge(s_["nmax_ready"], T + (s + 1))
                        e.activation(z[:, s % RING, 0:w], z[:, s % RING, 0:w], ACT.Exp,
                                     bias=nmax[:, s % 2:s % 2 + 1], scale=SCALE).then_inc(s_["exp_done"], 1)

        def maximum(e, kind, b, p, T, s):
            s_ = AA if kind == "A" else BB
            lo, hi, nm = mlo[:, s % 2:s % 2 + 1], mhi[:, s % 2:s % 2 + 1], nmax[:, s % 2:s % 2 + 1]
            e.wait_ge(s_["lo_read"], T + (s + 1))
            if s >= 2:
                e.wait_ge(s_["exp_done"], T + (s - 1))
            if kind == "A" or s % NT * P >= 2 * CH:
                e.wait_ge(s_["hi_read"], hbase(kind, T, b, p, 1) + (halves_before(kind, s, 1) + 1))
                if kind == "B":
                    settle(e)
                e.tensor_scalar(nm, lo, hi, -SCALE, ALU.max, ALU.mult).then_inc(s_["nmax_ready"], 1)
            else:
                if kind == "B":
                    settle(e)
                e.tensor_scalar(nm, lo, -SCALE, None, ALU.mult).then_inc(s_["nmax_ready"], 1)

        def pool_attention(e, b, kind):
            with e.Fori(0, nh // HB) as p:
                T = e.snap(b * (nh * NT) + p * G)
                for s in range(G):
                    maximum(e, kind, b, p, T, s)

        def dve_attention(e, b, kind):
            s_ = AA if kind == "A" else BB
            lag = LAG[kind]
            if kind == "A":
                rb = e.snap(b * (nh * NT + AHEAD))
                for t in range(AHEAD):
                    move_strip(e, e.tensor_copy, 3, t, rb, 0)
            def normalise(t):
                if t % OB != OB - 1:
                    return
                e.wait_ge(s_["comb_done"], U + (t // OB + 1))
                e.reciprocal(rsum[:, :], on[:, :, HD]).then_inc(s_["rcp"], 1)
                e.wait_ge(s_["rcp"], U + (t // OB + 1))
                t0 = t % NT - OB + 1
                e.tensor_tensor(attn[:, t0:t0 + OB, bass.ds(p * (HB * HD) + t // NT * HD, HD)], on[:, :, 0:HD],
                                rsum[:, :].rearrange("p (o w) -> p o w", w=1).to_broadcast([P, OB, HD]),
                                ALU.mult).then_inc(s_["out_read"], 1)

            with e.Fori(0, nh // HB) as p:
                T = e.snap(b * (nh * NT) + p * G)
                U = e.snap(b * (nh * NT // OB) + p * (G // OB))
                if kind == "A":
                    rb = e.snap(b * (nh * NT + AHEAD) + p * G)
                    wb = e.snap(b * (16 * (nh * 4 + 1)) + p * (16 * G // RING))
                    lb = e.snap(b * (16 * (nh * 4 + 1)) + p * (16 * G // RING))
                for s in range(G + lag + 1):
                    if s < G:
                        width = S if kind == "A" else (s % NT + 1) * P
                        if kind == "A":
                            e.wait_ge(strip_in[s % RING], lb + 16 * (s // RING + 1))
                        elif s >= RING:
                            wait_chunk(e, b, p, s - RING, (s - RING) % NT // 4)
                        lo, hi = mlo[:, s % 2:s % 2 + 1], mhi[:, s % 2:s % 2 + 1]
                        if s >= 2:
                            e.wait_ge(s_["nmax_ready"], T + (s - 1))
                        halves = halves_of(kind, s)
                        for half, ready, read in halves:
                            first = read == "lo_read"
                            mx = lo if first else hi
                            c0 = 0 if first else 2 * CH
                            c1 = min(width, c0 + 2 * CH)
                            p0 = half * 2 * CH
                            e.wait_ge(s_[ready], hbase(kind, T, b, p, 1 - first) + (halves_before(kind, s, 1 - first) + 1))
                            settle(e)
                            zs = z[:, s % RING, c0:c1]
                            add = zs if kind == "A" else mask[:, S - width + c0:S - width + c1]
                            e.tensor_tensor_reduce(out=zs, in0=scf[:, p0:p0 + c1 - c0], in1=add, scale=1.0, scalar=-3.0e38,
                                                   op0=ALU.add, op1=ALU.max, accum_out=mx).then_inc(s_[read], 1)
                        if kind == "A":
                            maximum(e, kind, b, p, T, s)
                    if s > lag:
                        t = s - lag - 1
                        ng = 4 if kind == "A" else min(4, t % NT + 1)
                        e.wait_ge(s_["pv_done"], T + (t + 1))
                        e.tensor_copy(po_sb[0:32 * ng, t % OB, :], po[0:32 * ng, :]).then_inc(s_["po_copied"], 1)
                    if kind == "A" and s < G:
                        move_strip(e, e.tensor_copy, 3, s + AHEAD, rb, wb)
                    if lag <= s < G + lag:
                        t = s - lag
                        if t >= 2:
                            e.wait_ge(s_["pv_done"], T + (t - 1))
                        if kind == "A":
                            for q in P_BY_DVE:
                                e.wait_ge(s_[f"pt_full{q}"], T + (t + 1))
                                e.tensor_copy(pT[:, t % 2, q * CH:(q + 1) * CH],
                                              rg[:, P_BANK[q], :]).then_inc(s_[f"pt_free{q}"], 1)
                        else:
                            nblk = t % NT + 1
                            q = 2 if nblk > 8 else 1
                            c0 = q * CH
                            w = min(nblk * P, 3 * CH) - c0
                            if w > 0:
                                wait_chunk(e, b, p, t, q)
                                e.tensor_copy(pT[:, t % 2, c0:c0 + w],
                                              rg[:, c0 // CH, 0:w]).then_inc(s_["pt_by_dve"], 1)
                            else:
                                e.memset(idle[:, :], 0.0).then_inc(s_["pt_by_dve"], 1)
                    if s > lag:
                        normalise(s - lag - 1)

        def load_parts(e, dst, col0, src, h, keys, done):
            at = 0
            for first, reps, n in (((0, 3, 1), (1, 2, 1), (2, 1, 1)) if keys else ((0, 1, 3), (0, 1, 2), (0, 1, 1))):
                rows_ = reps * n * HD
                s2 = src[bass.ds(h, 1), first * HD:(first + n) * HD, :].rearrange("a r s -> (a r) s")
                if keys:
                    for r in range(reps):
                        e.dma_start(dst[at:at + HD, col0:col0 + S], s2).then_inc(done, 16)
                        at += HD
                else:
                    e.dma_start(dst[at:at + rows_, col0:col0 + S], s2).then_inc(done, 16)
                    at += rows_

        def sp_attention(e, b, kind):
            s_ = AA if kind == "A" else BB

            def load_qk(h, hd):
                load_parts(e, qu_s[hd], 0, qu_d, h, False, s_[f"qk_loaded{hd}"])
                load_parts(e, k_s[hd], 0, k_d, h, True, s_[f"qk_loaded{hd}"])

            def load_qv(h, hd):
                load_parts(e, qv_s[hd], 0, qv_d, h, False, qv_loaded[hd])
                load_parts(e, pos_s[hd], 1, pos_d, h, True, qv_loaded[hd])

            def load_v(h, hd):
                e.dma_start(v_s[hd].rearrange("p t w -> p (t w)"),
                            v_d[bass.ds(h, 1)].rearrange("a p w -> (a p) w")).then_inc(s_[f"v_loaded{hd}"], 16)

            def strip_write(t, rb, db):
                k = t % RING
                for v in (e.snap(rb + (t + 1)),):
                    d = e.snap(db + 16 * (t // RING)) if t >= RING else None
                    e.wait_ge(r_free[4], v)
                    e.wait_ge(r_free[3], v)
                    if d is not None:
                        e.wait_ge(strip_in[k], d)
                    settle(e)
                e.dma_start(strip_d[k], strips[:, k * STRIP:(k + 1) * STRIP]).then_inc(strip_out[k], 16)

            def strip_read(t, T, db):
                k = t % RING
                d = e.snap(db + 16 * (t // RING + 1))
                v = e.snap(T + (t - RING + 1)) if t >= RING else None
                e.wait_ge(strip_out[k], d)
                settle(e)
                if v is not None:
                    e.wait_ge(s_["pt_full3"], v)
                settle(e)
                skewed = bass.AP(tensor=strip_d.tensor, offset=k * P * STRIP + P - 1, ap=[[STRIP - 1, P], [1, S]])
                e.dma_start(z[:, k, :], skewed).then_inc(strip_in[k], 16)

            def load_next(p, T, hd):
                if hd:
                    v = e.snap(T + hd * NT)
                    e.wait_ge(s_["pv_done"], v)
                    settle(e)
                h = e.snap(p * HB + (hd + 1))
                load_qk(h, (hd + 1) % NB)
                load_v(h, (hd + 1) % NB)

            load_qk(0, 0)
            load_v(0, 0)
            if kind == "A":
                load_qv(0, 0)
                load_qv(1, 1)
                rb = e.snap(b * (nh * NT + AHEAD))
                db = e.snap(b * (16 * (nh * 4 + 1)))
                for t in range(AHEAD + 1):
                    if t < AHEAD:
                        strip_write(t, rb, db)
                    if t >= 1:
                        strip_read(t - 1, 0, db)
            with e.Fori(0, nh // HB) as p:
                T = e.snap(b * (nh * NT) + p * G)
                if kind == "A":
                    rb = e.snap(b * (nh * NT + AHEAD) + p * G)
                    db = e.snap(b * (16 * (nh * 4 + 1)) + p * (16 * G // RING))
                v = e.snap(T + 1)
                e.wait_ge(s_["lo_ready"], v)
                settle(e)
                for s in range(G if kind == "A" else 0):
                    if s % NT == NT - AHEAD:
                        r = e.snap(rb + (s + AHEAD))
                        e.wait_ge(r_full[4], r)
                        settle(e)
                        load_qv(e.snap(p * HB + (s // NT + 2)), s // NT % NB)
                    strip_write(s + AHEAD, rb, db)
                    if s >= 2:
                        strip_read(s + 2, T, db)
                    if s % NT == 4:
                        load_next(p, T, s // NT)
                if kind == "A":
                    for t in (G + 2, G + 3):
                        strip_read(t, T, db)
                if kind == "B":
                    for hd in range(HB):
                        load_next(p, T, hd)
            if kind == "A":
                db = e.snap(b * (16 * (nh * 4 + 1)) + 16 * (nh * 4 + 1))
                for k in range(RING):
                    e.wait_ge(strip_in[k], db)
                v = e.snap(b * (QK_INC * (nh // NB + 1)) + QK_INC * (nh // NB + 1))
                for hd in range(NB):
                    e.wait_ge(qv_loaded[hd], v)
                    settle(e)
            for name, per in (("qk_loaded", QK_INC), ("v_loaded", 16)):
                for hd in range(NB):
                    v = e.snap(b * (per * loads_of(hd)) + per * loads_of(hd))
                    e.wait_ge(s_[f"{name}{hd}"], v)
                    settle(e)

        def oc(b, kind):
            return b * (2 * NT) + (NT if kind == "B" else 0)

        def pe_out(e, b, kind):
            w = wA if kind == "A" else wB
            base = e.snap(oc(b, kind))

            def tr(t):
                if t >= 2:
                    e.wait_ge(oo_T, base + (t - 1))
                for m in range(KT):
                    mm = e.transpose(rg[:, t % 2, m * P:(m + 1) * P], attn[:, t, m * P:(m + 1) * P], ident[:, :])
                mm.then_inc(oo_tr, 1)

            tr(0)
            for t in range(NT):
                if t + 1 < NT:
                    tr(t + 1)
                e.wait_ge(oo_T, base + (t + 1))
                if t >= 4:
                    e.wait_ge(oo_sum, base + (t - 3))
                for k in range(KT):
                    mm = e.matmul(sc[:, t % 4, 0:D], aoT[:, t % 2, k, :], w[:, 3, k, :], start=k == 0,
                                  stop=k == KT - 1)
                mm.then_inc(oo_ready, 1)

        def act_out(e, b, kind):
            base = e.snap(oc(b, kind))
            for t in range(NT):
                e.wait_ge(oo_tr, base + (t + 1))
                if t >= 2:
                    e.wait_ge(oo_ready, base + (t - 1))
                e.activation(aoT[:, t % 2, :, :], rg[:, t % 2, 0:D].rearrange("p (k c) -> p k c", k=KT),
                             ACT.Copy).then_inc(oo_T, 1)

        def dve_out(e, b, kind):
            k = 1 if kind == "A" else 3
            base = e.snap(oc(b, kind))
            for t in range(NT):
                e.wait_ge(oo_ready, base + (t + 1))
                e.tensor_tensor(x_res[:, t, :], sc[:, t % 4, 0:D], x_res[:, t, :], ALU.add).then_inc(oo_sum, 1)
                stats_behind(e, b, k, t, oo_added, base)
            for t in (NT, NT + 1):
                stats_behind(e, b, k, t, oo_added, base)

        def pool_out(e, b, kind):
            base = e.snap(oc(b, kind))
            for t in range(NT):
                e.wait_ge(oo_sum, base + (t + 1))
                e.tensor_tensor(x_res[:, t, :], x_res[:, t, :], rows[:, ROWS["bo" if kind == "A" else "Bbo"], :],
                                ALU.add).then_inc(oo_added, 1)

        def fc(b, k, per):
            return b * (2 * per) + k * per

        def norm_after(n):
            return (QT + n // 4 * 3 + n % 4,) if n < 2 * NI and n % 4 < 3 else ()

        def pe_ffn(e, b, k2):
            hb = e.snap(fc(b, k2, NC * NI))
            tb = e.snap(fc(b, k2, NT))

            def up(c):
                for i in range(NI):
                    n = c * NI + i
                    if n >= 4:
                        e.wait_ge(ff_relu, hb + (n - 3))
                    for k in range(KT):
                        mm = e.matmul(sc[:, n % 4, :], w1[:, k, i * P:(i + 1) * P], xnT[:, k, c * CH:(c + 1) * CH],
                                      start=k == 0, stop=k == KT - 1)
                    mm.then_inc(ff_h, 1)
                    pe_norm_tiles(e, b, 2 * k2 + 1, norm_after(n))

            def down(c):
                e.wait_ge(ff_relu, hb + (c + 1) * NI)
                for t in range(4 * c, 4 * c + 4):
                    if t >= 3:
                        e.wait_ge(ff_sum, tb + (t - 2))
                    for i in range(NI):
                        mm = e.matmul(rg[:, t % 3, 0:D], hT[c % 2][:, i, (t - 4 * c) * P:(t - 4 * c + 1) * P],
                                      w2[:, i, :], start=i == 0, stop=i == NI - 1)
                    mm.then_inc(ff_ready, 1)

            k = 2 * k2 + 1
            pe_norm_tiles(e, b, k, range(QT))
            for c in range(2):
                wait_norm(e, b, k, c)
                up(c)
            wait_norm(e, b, k, NC - 1)
            down(0)
            for c in range(1, NC):
                if c + 1 < NC:
                    up(c + 1)
                down(c)

        def act_ffn(e, b, k2):
            hb = e.snap(fc(b, k2, NC * NI))
            tb = e.snap(fc(b, k2, NT))
            for c in range(NC):
                if c == 0:
                    act_norm_tiles(e, b, 2 * k2 + 1, range(QT))
                if c >= 2:
                    e.wait_ge(ff_ready, tb + 4 * (c - 1))
                for i in range(NI):
                    n = c * NI + i
                    e.wait_ge(ff_h, hb + (n + 1))
                    e.activation(hT[c % 2][:, i, :], sc[:, n % 4, :], ACT.Relu,
                                 bias=cols[:, COLS["b1"] + i:COLS["b1"] + i + 1]).then_inc(ff_relu, 1)
                    act_norm_tiles(e, b, 2 * k2 + 1, norm_after(n))

        def dve_ffn(e, b, k2):
            tb = e.snap(fc(b, k2, NT))
            dve_norm_tiles(e, b, 2 * k2 + 1)
            for t in range(NT):
                e.wait_ge(ff_ready, tb + (t + 1))
                e.tensor_tensor(x_res[:, t, :], rg[:, t % 3, 0:D], x_res[:, t, :], ALU.add).then_inc(ff_sum, 1)
                if k2 == 0:
                    stats_behind(e, b, 2, t, ff_added, tb)
            if k2 == 0:
                for t in (NT, NT + 1):
                    stats_behind(e, b, 2, t, ff_added, tb)

        def pool_ffn(e, b, k2):
            tb = e.snap(fc(b, k2, NT))
            for t in range(NT):
                e.wait_ge(ff_sum, tb + (t + 1))
                e.tensor_tensor(x_res[:, t, :], x_res[:, t, :], rows[:, ROWS["b2"], :], ALU.add).then_inc(ff_added, 1)

        block = ctx.enter_context(nc.Block())

        @block.sync
        def _(e):
            def load_x(i, c):
                e.dma_start(x_res[:, c * QT:(c + 1) * QT, :],
                            a["x"][bass.ds(i, 1)].rearrange("a (t p) n -> p (a t) n", p=P)[:, c * QT:(c + 1) * QT]
                            ).then_inc(x_loaded[c], 16)

            def wload(dst, src):
                e.dma_start(dst, src).then_inc(loaded, 16)

            for i, n in enumerate(("q", "k", "v", "o")):
                wload(wA[:, i], a["A_W" + n].rearrange("(k p) n -> p k n", p=P))
                wload(wB[:, i], a["B_W" + n + "T"].rearrange("(k p) n -> p k n", p=P))
            wload(wp[:, :, :], a["A_Wp"].rearrange("(k p) n -> p k n", p=P))
            wload(w1[:, :, :], a["W1"].rearrange("(k p) n -> p k n", p=P))
            wload(w2[:, :, :], a["W2"].rearrange("(k p) n -> p k n", p=P))
            wload(cols[:, :], a["cols"])
            wload(rows[:, :, :].rearrange("p r n -> p (r n)"),
                  a["rows"].rearrange("r n -> (r n)").rearrange("(a m) -> a m", a=1).to_broadcast([P, 5 * D]))
            wload(ident[:, :], a["ident"])
            wload(sel[:, :], a["sel"])
            wload(mask[:, S - P:S], a["tri"])
            wload(embT, a["embT"].rearrange("(k p) s -> p k s", p=P))
            zd = sem_zero
            e.wait_ge(zeroed, 8)
            for h in range(H, H + NB):
                for d in (qu_d, qv_d, k_d, pos_d):
                    e.dma_start(d[h], k_sb[0:PARTS * HD, :]).then_inc(zd, 16)
                e.dma_start(v_d[h], mask[:, 0:NT * VW]).then_inc(zd, 16)
            e.wait_ge(loaded, 16 * LOADS)
            e.wait_ge(zd, 16 * 5 * NB)
            sp_project(e, None, "pos")
            meet(e, None, 0)
            for c in range(NC):
                load_x(0, c)
            for c in range(NC):
                e.wait_ge(x_loaded[c], 16)
            with e.Fori(0, nb) as b0:
                b = b0
                meet_b(e, b, 1)
                sp_project(e, b, "A")
                sp_values(e, b, "A")
                meet_b(e, b, 2)
                sp_attention(e, b, "A")
                meet_b(e, b, 3)
                meet_b(e, b, 4)
                meet_b(e, b, 5)
                sp_project(e, b, "B")
                sp_values(e, b, "B")
                meet_b(e, b, 6)
                sp_attention(e, b, "B")
                meet_b(e, b, 7)
                meet_b(e, b, 8)
                for c in range(NC):
                    v = e.snap(fc(b, 1, NT) + QT * (c + 1))
                    e.wait_ge(ff_added, v)
                    settle(e)
                    e.dma_start(out[bass.ds(b0, 1)].rearrange("a (t p) n -> p (a t) n", p=P)[:, c * QT:(c + 1) * QT],
                                x_res[:, c * QT:(c + 1) * QT, :]).then_inc(stored[c], 16)
                b_next = e.snap((b0 + 1) % nb)
                for c in range(NC):
                    v = e.snap(b * 16 + 16)
                    e.wait_ge(stored[c], v)
                    settle(e)
                    load_x(b_next, c)
                for c in range(NC):
                    v = e.snap(b * 16 + 32)
                    e.wait_ge(x_loaded[c], v)
                    settle(e)
                meet_b(e, b, 9)
                settle(e)

        @block.gpsimd
        def _(e):
            e.memset(k_sb[:, :], 0.0).then_inc(zeroed, 1)
            for hd in range(NB):
                e.memset(qv_s[hd][:, S:S + 1], 0.0).then_inc(zeroed, 1)
                e.memset(pos_s[hd][:, 0:1], 0.0).then_inc(zeroed, 1)
            e.memset(mask[:, 0:S - P], 0.0).then_inc(zeroed, 1)
            e.memset(mhi[:, :], 0.0).then_inc(zeroed, 1)
            e.memset(mlo[:, :], 0.0).then_inc(zeroed, 1)
            e.wait_ge(loaded, 16 * LOADS)
            pool_project(e, None, "pos")
            meet(e, None, 0)
            with e.Fori(0, nb) as b:
                meet_b(e, b, 1)
                pool_project(e, b, "A")
                pool_values(e, b, "A")
                meet_b(e, b, 2)
                meet_b(e, b, 3)
                pool_out(e, b, "A")
                meet_b(e, b, 4)
                pool_ffn(e, b, 0)
                meet_b(e, b, 5)
                pool_project(e, b, "B")
                pool_values(e, b, "B")
                meet_b(e, b, 6)
                pool_attention(e, b, "B")
                meet_b(e, b, 7)
                pool_out(e, b, "B")
                meet_b(e, b, 8)
                pool_ffn(e, b, 1)
                meet_b(e, b, 9)

        @block.tensor
        def _(e):
            e.wait_ge(loaded, 16 * LOADS)
            pe_project(e, None, "pos", embT)
            meet(e, None, 0)
            with e.Fori(0, nb) as b:
                meet_b(e, b, 1)
                pe_project(e, b, "A", xnT)
                pe_values(e, b, "A")
                meet_b(e, b, 2)
                pe_attention(e, b, "A")
                meet_b(e, b, 3)
                pe_out(e, b, "A")
                meet_b(e, b, 4)
                pe_ffn(e, b, 0)
                meet_b(e, b, 5)
                pe_project(e, b, "B", xnT)
                pe_values(e, b, "B")
                meet_b(e, b, 6)
                pe_attention(e, b, "B")
                meet_b(e, b, 7)
                pe_out(e, b, "B")
                meet_b(e, b, 8)
                pe_ffn(e, b, 1)
                meet_b(e, b, 9)

        @block.scalar
        def _(e):
            e.wait_ge(loaded, 16 * LOADS)
            act_project(e, None, "pos")
            meet(e, None, 0)
            with e.Fori(0, nb) as b:
                meet_b(e, b, 1)
                act_norm(e, b, 0)
                act_project(e, b, "A")
                meet_b(e, b, 2)
                act_attention(e, b, "A")
                meet_b(e, b, 3)
                act_out(e, b, "A")
                meet_b(e, b, 4)
                act_norm(e, b, 1)
                act_ffn(e, b, 0)
                meet_b(e, b, 5)
                act_norm(e, b, 2)
                act_project(e, b, "B")
                meet_b(e, b, 6)
                act_attention(e, b, "B")
                meet_b(e, b, 7)
                act_out(e, b, "B")
                meet_b(e, b, 8)
                act_norm(e, b, 3)
                act_ffn(e, b, 1)
                meet_b(e, b, 9)

        @block.vector
        def _(e):
            e.wait_ge(loaded, 16 * LOADS)
            for dst, n in ((bqu, "u"), (bqv, "v")):
                e.tensor_tensor(dst[:, :], cols[:, COLS["bq"]:COLS["bq"] + KT], cols[:, COLS[n]:COLS[n] + KT],
                                ALU.add).then_inc(bias_ready, 1)
            dve_project(e, None, "pos")
            meet(e, None, 0)
            with e.Fori(0, nb) as b:
                meet_b(e, b, 1)
                dve_norm(e, b, 0)
                dve_project(e, b, "A")
                dve_values(e, b, "A")
                meet_b(e, b, 2)
                dve_attention(e, b, "A")
                meet_b(e, b, 3)
                dve_out(e, b, "A")
                meet_b(e, b, 4)
                dve_norm(e, b, 1)
                dve_ffn(e, b, 0)
                meet_b(e, b, 5)
                dve_norm(e, b, 2)
                dve_project(e, b, "B")
                dve_values(e, b, "B")
                meet_b(e, b, 6)
                dve_attention(e, b, "B")
                meet_b(e, b, 7)
                dve_out(e, b, "B")
                meet_b(e, b, 8)
                dve_norm(e, b, 3)
                dve_ffn(e, b, 1)
                meet_b(e, b, 9)


def constants():
    pos = np.arange(S, dtype=np.float32)
    idx = np.arange(D // 2, dtype=np.float32)
    inv_freq = np.float32(1.0) / np.float32(10000.0) ** (np.float32(2.0) * idx / np.float32(D))
    ang = pos[:, None] * inv_freq[None, :].astype(np.float32)
    emb = np.concatenate([np.sin(ang), np.cos(ang)], axis=-1).astype(np.float32)
    sel = np.zeros((P, VW), np.float32)
    for p in range(P):
        sel[p, p % VW] = 1.0
    tri = np.where(np.arange(P)[None, :] > np.arange(P)[:, None], NEG, 0.0).astype(np.float32)
    return {"embT": np.ascontiguousarray(emb.T), "ident": np.eye(P, dtype=np.float32), "sel": sel, "tri": tri}


def arrays_of(i):
    c = np.ascontiguousarray

    def two(x):
        return np.asarray(x).reshape(-1, P).T

    arr = {"x": c(i["L0_attn_a_x"])}
    for n in "qkvpo":
        arr["A_W" + n] = c(i["L0_attn_a_W" + n])
    for n in "qkvo":
        arr["B_W" + n + "T"] = c(np.asarray(i["L0_attn_b_W" + n]).T)
    arr["W1"] = c(i["L0_ffn_W1"])
    arr["W2"] = c(i["L0_ffn_W2"])
    arr["cols"] = c(np.concatenate([two(i[n]) for n in (
        "L0_attn_a_bq", "L0_attn_a_bk", "L0_attn_a_bp", "L0_attn_a_u", "L0_attn_a_v", "L0_attn_b_bq",
        "L0_attn_b_bk", "L0_ffn_b1")], axis=1))
    arr["rows"] = c(np.stack([np.asarray(i[n]) for n in (
        "L0_attn_a_bv", "L0_attn_a_bo", "L0_attn_b_bv", "L0_attn_b_bo", "L0_ffn_b2")]))
    arr.update(constants())
    return arr


def kernel(**inputs):
    import concourse.bacc as bacc
    from concourse.bass_utils import run_bass_kernel_spmd

    nc = bacc.Bacc("TRN2", target_bir_lowering=False, num_devices=1)
    arrays = {"in_" + n: v for n, v in arrays_of(inputs).items()}
    aps = {n[3:]: nc.dram_tensor(n, v.shape, mybir.dt.from_np(v.dtype), kind="ExternalInput").ap()
           for n, v in arrays.items()}
    shape = inputs["L0_attn_a_x"].shape
    out = nc.dram_tensor("out_0_dram", shape, F32, kind="ExternalOutput").ap()
    program(nc, aps, out)
    r = run_bass_kernel_spmd(nc, [arrays], core_ids=[0])
    return r.results[0]["out_0_dram"]
```
